# Optimizing a Trainium2 kernel written in Bass

```python
import numpy as np
import jax
import jax.numpy as jnp

def _softmax(x, axis=-1):
    return jax.nn.softmax(x, axis=axis)

def _gelu(x):
    return jax.nn.gelu(x, approximate=True)

def _silu(x):
    return jax.nn.silu(x)

def _sigmoid(x):
    return jax.nn.sigmoid(x)

def _layernorm(x, axis=-1, eps=1e-05):
    m = jnp.mean(x, axis=axis, keepdims=True)
    v = jnp.var(x, axis=axis, keepdims=True)
    return (x - m) / jnp.sqrt(v + eps)

def _scatter_add(tgt, idx, src, axis=0):
    return tgt.at[idx].add(src)

def _segment_sum(src, seg, n):
    return jax.ops.segment_sum(src, seg, n)
kernel_name = 'mk_xattn_ffn_d1_seqx_r8_dadb35'

def setup_inputs(seed: int=0):
    np.random.seed(seed)
    _w = jnp.asarray

    def _rec_inputs():
        import jax
        import jax.numpy as jnp
        _rk = jax.random.key(seed)
        x = 0.0003765 + 1 * jax.random.normal(jax.random.fold_in(_rk, 1), (8, 128, 256), jnp.float32)
        _lenS = 128 - jax.random.randint(jax.random.fold_in(_rk, 7), (8,), 0, max(1, 128 // 4) + 1, jnp.int32)
        _lenS2 = 128 - jax.random.randint(jax.random.fold_in(_rk, 8), (8,), 0, max(1, 128 // 4) + 1, jnp.int32)
        _ctx_2048P = jax.random.normal(jax.random.fold_in(_rk, 11), (8, 16, 256), jnp.float32)
        _ctx_2048c = jax.random.dirichlet(jax.random.fold_in(_rk, 511), 0.3 * jnp.ones((16,), jnp.float32), (8, 128))
        _ctx_2048t = jnp.einsum('bsk,bkd->bsd', _ctx_2048c, _ctx_2048P)
        _ctx_2048t = _ctx_2048t * jax.lax.rsqrt(jnp.mean(jnp.square(_ctx_2048t)) + 1e-12) * 0.953939
        ctx_2048 = -0.000292821 + 1.00034 * (_ctx_2048t + 0.3 * jax.random.normal(jax.random.fold_in(_rk, 611), (8, 128, 256), jnp.float32))
        return (x, ctx_2048)
    x, ctx_2048 = _rec_inputs()

    def _L0_xattn_setup():
        import jax, jax.numpy as jnp
        import numpy as np
        key = jax.random.key(seed)
        k1, k2, k3, k4, k5 = jax.random.split(key, 5)
        B, D_MODEL, L = (2, 128, 256)
        HEAD_DIM = 8
        H = D_MODEL // HEAD_DIM
        return {'k': jax.random.normal(k1, (B, D_MODEL, L), dtype=jnp.float32), 'v': jax.random.normal(k2, (B, D_MODEL, L), dtype=jnp.float32), 'q': jax.random.normal(k3, (B, D_MODEL, L), dtype=jnp.float32), 'ssm_kernel': jax.random.normal(k4, (H, L), dtype=jnp.float32), 'D': jax.random.normal(k5, (H,), dtype=jnp.float32), 'head_dim': HEAD_DIM}
    _L0_xattn_all = _L0_xattn_setup()
    _L0_xattn_in = {k: v for k, v in _L0_xattn_all.items() if k in ('ssm_kernel', 'D')}
    del _L0_xattn_all

    def _L0_ffn_setup():
        import jax, jax.numpy as jnp
        import numpy as np
        DIM = 256
        HID = 704
        ZERO_POINT = 128.0

        def _qlinear(x, wq, scale):
            W = (wq.astype(jnp.float32) - ZERO_POINT) * scale[:, None]
            return jnp.einsum('bsd,hd->bsh', x, W)
        key = jax.random.key(seed)
        ks = jax.random.split(key, 7)
        B, S = (4, 256)
        sg = jax.random.uniform(ks[1], (HID,)) * (0.02 / np.sqrt(DIM)) + 0.0001
        su = jax.random.uniform(ks[3], (HID,)) * (0.02 / np.sqrt(DIM)) + 0.0001
        sd = jax.random.uniform(ks[5], (DIM,)) * (0.02 / np.sqrt(HID)) + 0.0001
        return {'x': jax.random.normal(ks[0], (B, S, DIM), dtype=jnp.float32), 'wq_gate': jax.random.randint(ks[2], (HID, DIM), 0, 32, dtype=jnp.int32), 's_gate': sg, 'wq_up': jax.random.randint(ks[4], (HID, DIM), 0, 32, dtype=jnp.int32), 's_up': su, 'wq_down': jax.random.randint(ks[6], (DIM, HID), 0, 32, dtype=jnp.int32), 's_down': sd}
    _L0_ffn_all = _L0_ffn_setup()
    _L0_ffn_in = {k: v for k, v in _L0_ffn_all.items() if k in ('wq_gate', 's_gate', 'wq_up', 's_up', 'wq_down', 's_down')}
    del _L0_ffn_all
    return {'x': x, 'ctx_2048': ctx_2048, 'L0_xattn_ssm_kernel': _L0_xattn_in['ssm_kernel'], 'L0_xattn_D': _L0_xattn_in['D'], 'L0_ffn_wq_gate': _L0_ffn_in['wq_gate'], 'L0_ffn_s_gate': _L0_ffn_in['s_gate'], 'L0_ffn_wq_up': _L0_ffn_in['wq_up'], 'L0_ffn_s_up': _L0_ffn_in['s_up'], 'L0_ffn_wq_down': _L0_ffn_in['wq_down'], 'L0_ffn_s_down': _L0_ffn_in['s_down']}

def reference(x, ctx_2048, L0_xattn_ssm_kernel, L0_xattn_D, L0_ffn_wq_gate, L0_ffn_s_gate, L0_ffn_wq_up, L0_ffn_s_up, L0_ffn_wq_down, L0_ffn_s_down):
    import jax
    import jax.numpy as jnp

    def _L0_xattn_ref(k, v, q, ssm_kernel, D, head_dim):
        import jax, jax.numpy as jnp
        import numpy as np
        B, HD, L = k.shape
        H = HD // head_dim
        fft_size = 2 * L
        k_ = k.reshape(B, H, head_dim, L)
        v_ = v.reshape(B, H, head_dim, L)
        q_ = q.reshape(B, H, head_dim, L)
        kv = jnp.einsum('bhil,bhjl->bijhl', k_, v_)
        kv_f = jnp.fft.rfft(kv, n=fft_size)
        kernel_f = jnp.fft.rfft(ssm_kernel, n=fft_size)
        y = jnp.fft.irfft(kv_f * kernel_f, n=fft_size)[..., :L]
        out = y + kv * D[None, None, None, :, None]
        out = jnp.einsum('bijhl,bhil->bjhl', out, q_)
        out = jnp.transpose(out, (0, 2, 1, 3)).reshape(B, H * head_dim, L)
        return out.astype(k.dtype)

    def _L0_ffn_ref(x, wq_gate, s_gate, wq_up, s_up, wq_down, s_down):
        import jax, jax.numpy as jnp
        import numpy as np
        DIM = 256
        HID = 704
        ZERO_POINT = 128.0

        def _qlinear(x, wq, scale):
            W = (wq.astype(jnp.float32) - ZERO_POINT) * scale[:, None]
            return jnp.einsum('bsd,hd->bsh', x, W)
        gate = _qlinear(x, wq_gate, s_gate)
        gate = jax.nn.silu(gate)
        up = _qlinear(x, wq_up, s_up)
        return _qlinear(gate * up, wq_down, s_down)
    x = x + _L0_xattn_ref(ctx_2048, ctx_2048, _layernorm(x, axis=-1), L0_xattn_ssm_kernel, L0_xattn_D, 8)
    x = x + _L0_ffn_ref(_layernorm(x, axis=-1), L0_ffn_wq_gate, L0_ffn_s_gate, L0_ffn_wq_up, L0_ffn_s_up, L0_ffn_wq_down, L0_ffn_s_down)
    return x

_drawn_inputs = setup_inputs


def setup_inputs(seed=0):
    import zlib

    import numpy as np

    out = dict(_drawn_inputs(seed))
    spreads = {}
    factors = {'L0_ffn_s_gate': 8.0, 'L0_ffn_s_up': 8.0, 'L0_ffn_s_down': 8.0}
    for name, (base, spread) in spreads.items():
        noise = np.random.default_rng([zlib.crc32(name.encode()), seed]).standard_normal(out[name].shape)
        drawn = base * np.exp(spread * noise) if base else spread * noise
        out[name] = jnp.asarray(drawn.astype(out[name].dtype))
    for name, factor in factors.items():
        out[name] = (out[name] * factor).astype(out[name].dtype)
    return out
```

```python
from contextlib import ExitStack

import concourse.bass as bass
from concourse import mybir

F32 = mybir.dt.float32
F32R = mybir.dt.float32r
F16 = mybir.dt.float16
I32 = mybir.dt.int32
ALU = mybir.AluOpType
ACT = mybir.ActivationFunctionType

P = 128
B, H, C, L = 8, 16, 8, 256
HID = 704
ZERO_POINT = 128.0
EPS = 1e-5

HALVES = L // P
EXT = C + C // 2
PAIRS = C * (C // 2) + C // 2
COLS = B * PAIRS
TILE_HEADS = P // (B * C)
BLOCK_HEADS = 2 * TILE_HEADS
TILES = H // TILE_HEADS
BLOCKS = H // BLOCK_HEADS
ROWS = 2 * P
CHUNKS = -(-HID // P)

CHANNEL = B * TILE_HEADS
SPARE = 3 * CHANNEL
BACK = 4 * P + SPARE
CROSS = BACK + 3 * (P + SPARE)
TERMS = CROSS + P
SLOT_AT = [0, P, 2 * P, 3 * P, BACK, BACK + P + SPARE, BACK + 2 * (P + SPARE), CROSS]


def view(ap, offset, dims):
    return bass.AP(ap.tensor, ap.offset + offset, [list(ap.ap[0])] + [list(d) for d in dims])


def chunk_size(t):
    return min(P, HID - t * P)


def build(nc, x, ctx_ext, taps, skip, wg_t, s_gate, wu_t, s_up, wd_t, s_down, taps_pad, out):
    with ExitStack() as ctx:
        def sb(name, shape, dt=F32):
            return ctx.enter_context(nc.sbuf_tensor(name, shape, dt))

        def sem(name):
            return ctx.enter_context(nc.semaphore(name))

        x_sb = sb("x_sb", [P, TILES, L])
        k_ext = sb("k_ext", [P, H, HALVES, EXT * B])
        products = sb("products", [P, H, HALVES * COLS])
        toeplitz = sb("toeplitz", [P, BLOCK_HEADS, L])
        taps_sb = sb("taps_sb", [H, P + L])
        skip_sb = sb("skip_sb", [H, 1])
        ident = sb("ident", [P, P])
        q_rows = sb("q_rows", [P, 2, L])
        q_ext = sb("q_ext", [P, 2, TILE_HEADS * HALVES * EXT * B])
        terms = sb("terms", [P, 2, HALVES * TERMS])
        f_rows = sb("f_rows", [P, 2, L])
        f_hi = sb("f_hi", [P, HALVES, ROWS], F16)
        f_lo = sb("f_lo", [P, HALVES, ROWS], F16)
        stats_q = sb("stats_q", [P, TILES, 6])
        moments_q = sb("moments_q", [P, TILES, 2])
        variance_q = sb("variance_q", [P, TILES])
        rstd_q = sb("rstd_q", [P, TILES])
        stats_f = sb("stats_f", [P, 2, 6])
        moments_f = sb("moments_f", [P, 2, 2])
        variance_f = sb("variance_f", [P, 2])
        rstd_f = sb("rstd_f", [P, 2])
        minus_half = sb("minus_half", [P, TILES])
        wg_int = sb("wg_int", [P, HALVES, HID], I32)
        wu_int = sb("wu_int", [P, HALVES, HID], I32)
        wd_int = sb("wd_int", [P, CHUNKS, L], I32)
        wg = sb("wg", [P, HALVES, HID], F16)
        wu = sb("wu", [P, HALVES, HID], F16)
        wd = sb("wd", [P, CHUNKS, L], F32R)
        sg_sb = sb("sg_sb", [P, CHUNKS])
        su_sb = sb("su_sb", [P, CHUNKS])
        sd_sb = sb("sd_sb", [P, L])
        gate_act = sb("gate_act", [P, 2, ROWS])
        hidden = sb("hidden", [P, 2, ROWS])
        h_hi = sb("h_hi", [P, 3, ROWS], F32R)
        h_lo = sb("h_lo", [P, 3, ROWS], F32R)
        ffn_out = sb("ffn_out", [P, 2, L])

        BANK = 512
        conv = [ctx.enter_context(nc.psum_tensor(f"conv{n}", [P, 2 * BANK], F32)) for n in range(2)]
        HALF0 = BANK - COLS
        sums = ctx.enter_context(nc.psum_tensor("sums", [P, BANK], F32))
        gate_up = [ctx.enter_context(nc.psum_tensor(f"gate_up{n}", [P, 2, ROWS], F32)) for n in range(2)]
        down = ctx.enter_context(nc.psum_tensor("down", [P, 2, L], F32))

        taps_loaded = sem("taps_loaded")
        taps_zeroed = sem("taps_zeroed")
        taps_ready = sem("taps_ready")
        taps_stored = sem("taps_stored")
        toeplitz_loaded = [sem(f"toeplitz_loaded{s}") for s in range(BLOCK_HEADS)]
        x0_loaded, x_loaded = sem("x0_loaded"), sem("x_loaded")
        k0_loaded, k_loaded = sem("k0_loaded"), sem("k_loaded")
        w_loaded = sem("w_loaded")
        w_ready = sem("w_ready")
        ident_zeroed, ident_ready = sem("ident_zeroed"), sem("ident_ready")
        products_ready = sem("products_ready")
        conv_done = sem("conv_done")
        half_ready = sem("half_ready")
        q_stats = sem("q_stats")
        q_moments = sem("q_moments")
        q_variance = sem("q_variance")
        q_rstd = sem("q_rstd")
        q_normed = sem("q_normed")
        q_turned = sem("q_turned")
        q_ready = sem("q_ready")
        terms_ready = sem("terms_ready")
        summed = sem("summed")
        x1_steps = sem("x1_steps")
        f_rstd = sem("f_rstd")
        f_normed = sem("f_normed")
        f_turned = sem("f_turned")
        f_hi_ready = sem("f_hi_ready")
        f_lo_ready = sem("f_lo_ready")
        gate_up_done = sem("gate_up_done")
        gate_act_ready = sem("gate_act_ready")
        hidden_ready = sem("hidden_ready")
        h_hi_ready = sem("h_hi_ready")
        h_lo_ready = sem("h_lo_ready")
        chunk_down = sem("chunk_down")
        waited = sem("waited")
        out_scaled = sem("out_scaled")
        out_ready = sem("out_ready")
        out_stored = sem("out_stored")

        credited = (chunk_down, hidden_ready, h_lo_ready, out_ready, out_scaled)

        def wait(eng, semaphore, per_block, block, offset):
            credit = 1 if semaphore in credited else 0
            if not isinstance(block, int) or per_block * block + offset > 0:
                eng.wait_ge(semaphore, block * per_block + (offset + credit))

        def wait_place(eng, semaphore, per_block, block, offset):
            wait(eng, semaphore, per_block, block, offset if isinstance(block, int) else max(offset, 0))

        block = ctx.enter_context(nc.Block())

        @block.sync
        def _(sp):
            def load_toeplitz(i, s):
                src = bass.AP(taps_pad.tensor, (i * BLOCK_HEADS + s) * (P + L) + 1, [[1, P], [1, L]])
                sp.dma_start(toeplitz[:, s, :], src).then_inc(toeplitz_loaded[s], 16)

            def store(i, r):
                wait(sp, out_ready, 2, i, r + 1)
                sp.dma_start(out_at(i, r), x_at(i, r)).then_inc(out_stored, 16)

            def out_at(i, r):
                return out[bass.ds((i * 2 + r) * P, P), :]

            def x_at(i, r):
                return x_sb[:, bass.ds(i * 2 + r, 1), :]

            sp.dma_start(taps_sb[:, P:], taps).then_inc(taps_loaded, 16)
            sp.dma_start(skip_sb[:, :], skip).then_inc(taps_loaded, 16)
            sp.dma_start(k_ext[:, 0:BLOCK_HEADS], ctx_ext[:, 0:BLOCK_HEADS]).then_inc(k0_loaded, 16)
            sp.wait_ge(taps_ready, 1)
            sp.dma_start(taps_pad, taps_sb[:, :]).then_inc(taps_stored, 16)
            sp.wait_ge(taps_stored, 16)
            for s in range(BLOCK_HEADS):
                load_toeplitz(0, s)
            sp.dma_start(k_ext[:, BLOCK_HEADS:], ctx_ext[:, BLOCK_HEADS:]).then_inc(k_loaded, 16)
            def reload(i):
                for s in range(BLOCK_HEADS):
                    wait(sp, conv_done, BLOCK_HEADS, i, s + 1)
                    load_toeplitz(i + 1, s)

            reload(0)
            with sp.Fori(1, BLOCKS - 1) as i:
                reload(i)
                store(i - 1, 0)
                store(i - 1, 1)
            for i in range(BLOCKS - 2, BLOCKS):
                store(i, 0)
                store(i, 1)
            sp.wait_ge(out_stored, 16 * TILES)

        @block.gpsimd
        def _(pool):
            for semaphore in credited:
                pool.sem_inc(semaphore, 1)
            nc.gpsimd.memset(minus_half[:, :], -0.5).then_inc(half_ready, 1)
            nc.gpsimd.memset(ident[:, :], 0.0).then_inc(ident_zeroed, 1)
            pool.wait_ge(half_ready, 1)
            pool.wait_ge(ident_zeroed, 1)
            nc.gpsimd.affine_select(out=ident[:, :], in_=ident[:, :], compare_op=ALU.not_equal, fill=1.0,
                                    base=0, pattern=[[-1, P]], channel_multiplier=1).then_inc(ident_ready, 1)

            def multiply_pairs(n):
                k = k_ext[:, bass.ds(n, 1)]
                o = products[:, bass.ds(n, 1)]
                nc.gpsimd.tensor_tensor(
                    view(o, 0, [[COLS, HALVES], [C * B, 4], [1, C * B]]),
                    view(k, 0, [[EXT * B, HALVES], [0, 4], [1, C * B]]),
                    view(k, 0, [[EXT * B, HALVES], [B, 4], [1, C * B]]), ALU.mult)
                nc.gpsimd.tensor_tensor(
                    view(o, 4 * C * B, [[COLS, HALVES], [1, 4 * B]]),
                    view(k, 0, [[EXT * B, HALVES], [1, 4 * B]]),
                    view(k, 4 * B, [[EXT * B, HALVES], [1, 4 * B]]), ALU.mult).then_inc(products_ready, 1)

            def root(base, power, result, done):
                nc.gpsimd.tensor_tensor(result, base, power, ALU.pow).then_inc(done, 1)

            def root_q(tiles, count):
                pool.wait_ge(q_variance, count)
                root(variance_q[:, tiles], minus_half[:, tiles], rstd_q[:, tiles], q_rstd)

            def root_f(i, r):
                wait(pool, x1_steps, 8, i, 4 * r + 4)
                wait(pool, f_normed, 2, i, r - 1)
                root(variance_f[:, r:r + 1], minus_half[:, 0:1], rstd_f[:, r:r + 1], f_rstd)

            def low_hidden(i, t):
                m = chunk_size(t)
                wait(pool, h_hi_ready, CHUNKS, i, t + 1)
                wait_place(pool, chunk_down, CHUNKS, i, t - 2)
                nc.gpsimd.tensor_tensor(h_lo[0:m, t % 3, :], hidden[0:m, t % 2, :], h_hi[0:m, t % 3, :],
                                        ALU.subtract).then_inc(h_lo_ready, 1)

            def add_ffn(i, r):
                x1 = x_sb[:, bass.ds(i * 2 + r, 1), :]
                wait(pool, out_scaled, 2, i, r + 1)
                nc.gpsimd.tensor_tensor(x1, x1, ffn_out[:, r:r + 1, :], ALU.add).then_inc(out_ready, 1)

            def step(i, attention, ffn, more):
                following = BLOCK_HEADS * i + BLOCK_HEADS
                if ffn:
                    root_f(i - 1, 1)
                if more:
                    multiply_pairs(following)
                    multiply_pairs(following + 1)
                if ffn:
                    low_hidden(i - 1, 0)
                    low_hidden(i - 1, 1)
                if more:
                    multiply_pairs(following + 2)
                if ffn:
                    low_hidden(i - 1, 2)
                    low_hidden(i - 1, 3)
                    low_hidden(i - 1, 4)
                if more:
                    multiply_pairs(following + 3)
                if ffn:
                    low_hidden(i - 1, 5)
                if attention:
                    root_f(i, 0)
                if ffn:
                    add_ffn(i - 1, 0)
                    add_ffn(i - 1, 1)

            pool.wait_ge(k0_loaded, 16)
            multiply_pairs(0)
            root_q(slice(0, 2), 1)
            multiply_pairs(1)
            multiply_pairs(2)
            multiply_pairs(3)
            pool.wait_ge(k_loaded, 16)
            step(0, True, False, True)
            root_q(slice(2, TILES), 2)
            with pool.Fori(1, BLOCKS - 1) as i:
                step(i, True, True, True)
            step(BLOCKS - 1, True, True, False)
            step(BLOCKS, False, True, False)

        @block.scalar
        def _(act):
            def evict_q(i, r):
                if True:
                    wait(act, q_turned, 2, i, r + 1)
                    wait(act, terms_ready, BLOCK_HEADS, i, 2 * r + 2 - BLOCK_HEADS)
                    o, src = q_ext[:, r, :], down[:, 0, :]
                    half, head = EXT * B, HALVES * EXT * B
                    nc.scalar.activation(
                        view(o, 0, [[head, TILE_HEADS], [half, HALVES], [1, C * B]]),
                        view(src, 0, [[1, TILE_HEADS], [P, HALVES], [TILE_HEADS, C * B]]), ACT.Copy)
                    last = nc.scalar.activation(
                        view(o, C * B, [[head, TILE_HEADS], [half, HALVES], [1, 4 * B]]),
                        view(src, 0, [[1, TILE_HEADS], [P, HALVES], [TILE_HEADS, 4 * B]]), ACT.Copy)
                    last.then_inc(q_ready, 1)

            def evict_f(r, i):
                wait(act, f_turned, 2, i, r + 1)
                nc.scalar.activation(f_hi[:, :, r * P:(r + 1) * P],
                                     down[:, 0, :].rearrange("p (c n) -> p c n", c=HALVES),
                                     ACT.Copy).then_inc(f_hi_ready, 1)

            def gate(i, t):
                m = chunk_size(t)
                wait(act, gate_up_done, CHUNKS, i, t + 1)
                wait_place(act, hidden_ready, CHUNKS, i, t - 1)
                nc.scalar.activation(gate_act[0:m, t % 2, :], gate_up[t % 2][0:m, 0, :], ACT.Silu,
                                     scale=sg_sb[0:m, t:t + 1]).then_inc(gate_act_ready, 1)

            def hidden_high(i, t):
                m = chunk_size(t)
                wait(act, hidden_ready, CHUNKS, i, t + 1)
                wait_place(act, chunk_down, CHUNKS, i, t - 2)
                nc.scalar.activation(h_hi[0:m, t % 3, :], hidden[0:m, t % 2, :], ACT.Copy).then_inc(h_hi_ready, 1)

            def load_weights():
                full = (CHUNKS - 1) * P
                act.dma_start(wg_int[:, :, :], wg_t.rearrange("(c p) n -> p c n", p=P)).then_inc(w_loaded, 16)
                act.dma_start(wu_int[:, :, :], wu_t.rearrange("(c p) n -> p c n", p=P)).then_inc(w_loaded, 16)
                act.dma_start(wd_int[:, 0:CHUNKS - 1, :],
                              wd_t[0:full, :].rearrange("(t p) n -> p t n", p=P)).then_inc(w_loaded, 16)
                act.dma_start(wd_int[0:HID - full, CHUNKS - 1, :], wd_t[full:HID, :]).then_inc(w_loaded, 16)
                act.dma_start(sg_sb[:, :], s_gate).then_inc(w_loaded, 16)
                act.dma_start(su_sb[:, :], s_up).then_inc(w_loaded, 16)
                act.dma_start(sd_sb[:, :], s_down.partition_broadcast(P)).then_inc(w_loaded, 16)

            def convert_weights():
                act.wait_ge(w_loaded, 7 * 16)
                nc.scalar.activation(wg[:, :, :], wg_int[:, :, :], ACT.Copy, bias=-ZERO_POINT)
                nc.scalar.activation(wu[:, :, :], wu_int[:, :, :], ACT.Copy, bias=-ZERO_POINT)
                nc.scalar.activation(wd[:, 0:CHUNKS - 1, :], wd_int[:, 0:CHUNKS - 1, :], ACT.Copy, bias=-ZERO_POINT)
                m = chunk_size(CHUNKS - 1)
                nc.scalar.activation(wd[0:m, CHUNKS - 1, :], wd_int[0:m, CHUNKS - 1, :], ACT.Copy,
                                     bias=-ZERO_POINT).then_inc(w_ready, 1)

            def step(i, attention, ffn):
                if attention:
                    evict_q(i, 0)
                if ffn:
                    evict_f(0, i - 1)
                    evict_f(1, i - 1)
                    gate(i - 1, 0)
                if attention:
                    evict_q(i, 1)
                if ffn:
                    gate(i - 1, 1)
                    hidden_high(i - 1, 0)
                    hidden_high(i - 1, 1)
                    for t in range(2, CHUNKS):
                        gate(i - 1, t)
                        hidden_high(i - 1, t)

            act.dma_start(x_sb[:, 0:2, :], x[0:ROWS, :].rearrange("(t p) l -> p t l", p=P)).then_inc(x0_loaded, 16)
            act.dma_start(x_sb[:, 2:TILES, :], x[ROWS:, :].rearrange("(t p) l -> p t l", p=P)).then_inc(x_loaded, 16)
            load_weights()
            nc.scalar.preload_act_table(ACT.Silu)
            step(0, True, False)
            convert_weights()
            with act.Fori(1, BLOCKS) as i:
                step(i, True, True)
            step(BLOCKS, False, True)

        @block.vector
        def _(dve):
            dve.memset(taps_sb[:, 0:P], 0.0).then_inc(taps_zeroed, 1)
            dve.wait_ge(taps_loaded, 32)
            dve.wait_ge(taps_zeroed, 1)
            dve.tensor_tensor(taps_sb[:, P:P + 1], taps_sb[:, P:P + 1], skip_sb[:, :], ALU.add).then_inc(taps_ready, 1)

            def tile_of(i, r):
                return x_sb[:, bass.ds(i * 2 + r, 1), :].rearrange("p t l -> p (t l)")

            def variances_q(tiles, count):
                for t in tiles:
                    last = dve.bn_stats(stats_q[:, t, :], x_sb[:, t, :])
                last.then_inc(q_stats, 1)
                dve.wait_ge(q_stats, count)
                for t in tiles:
                    last = dve.bn_aggr(moments_q[:, t, :], stats_q[:, t, :])
                last.then_inc(q_moments, 1)
                dve.wait_ge(q_moments, count)
                dve.tensor_scalar(variance_q[:, tiles[0]:tiles[-1] + 1],
                                  view(moments_q[:, tiles[0], :], 1, [[2, len(tiles)]]), EPS, None,
                                  ALU.add).then_inc(q_variance, 1)

            def norm_q(i, r):
                if True:
                    tile = bass.ds(i * 2 + r, 1)
                    wait(dve, q_turned, 2, i, r - 1)
                    dve.tensor_scalar(q_rows[:, r, :], tile_of(i, r),
                                      moments_q[:, tile, 0:1].rearrange("p t c -> p (t c)"), rstd_q[:, tile],
                                      ALU.subtract, ALU.mult).then_inc(q_normed, 1)

            def wait_apart(semaphore, per_block, i, offset):
                wait(dve, semaphore, per_block, i, offset)
                dve.sem_inc(waited, 1)

            def add_attention(i, r):
                x1 = tile_of(i, r)
                wait(dve, summed, 2, i, r + 1)
                dve.tensor_tensor(x1, x1, sums[:, 0:L], ALU.add).then_inc(x1_steps, 1)
                wait_apart(x1_steps, 8, i, 4 * r + 1)
                dve.bn_stats(stats_f[:, r, :], x1).then_inc(x1_steps, 1)
                wait_apart(x1_steps, 8, i, 4 * r + 2)
                dve.bn_aggr(moments_f[:, r, :], stats_f[:, r, :]).then_inc(x1_steps, 1)
                wait(dve, x1_steps, 8, i, 4 * r + 3)
                dve.tensor_scalar(variance_f[:, r:r + 1], moments_f[:, r, 1:2], EPS, None,
                                  ALU.add).then_inc(x1_steps, 1)

            def norm_f(i, r):
                wait(dve, f_rstd, 2, i, r + 1)
                wait(dve, f_turned, 2, i, r - 1)
                dve.tensor_scalar(f_rows[:, r, :], tile_of(i, r), moments_f[:, r, 0:1], rstd_f[:, r:r + 1],
                                  ALU.subtract, ALU.mult).then_inc(f_normed, 1)

            def multiply_terms(i, s):
                r, h = s // TILE_HEADS, s % TILE_HEADS
                wait(dve, conv_done, BLOCK_HEADS, i, s + 1)
                if h == 0:
                    wait(dve, q_ready, 2, i, r + 1)
                    wait(dve, summed, 2, i, r - 1)
                y = conv[s % 2][:, :]
                q = q_ext[:, r, :]
                z = terms[:, r, :]
                half = EXT * B
                q0 = h * HALVES * half
                to = TILE_HEADS
                dve.tensor_tensor(view(z, h, [[TERMS, HALVES], [P, 4], [to, C * B]]),
                                  view(y, HALF0, [[COLS, HALVES], [C * B, 4], [1, C * B]]),
                                  view(q, q0, [[half, HALVES], [B, 4], [1, C * B]]), ALU.mult)
                dve.tensor_tensor(view(z, h + BACK + CHANNEL,
                                       [[TERMS, HALVES], [P + SPARE + CHANNEL, 3], [to, C * B]]),
                                  view(y, HALF0 + C * B, [[COLS, HALVES], [C * B, 3], [1, C * B]]),
                                  view(q, q0, [[half, HALVES], [0, 3], [1, C * B]]), ALU.mult)
                dve.tensor_tensor(view(z, h + BACK - 2 * CHANNEL,
                                       [[TERMS, HALVES], [P + SPARE + CHANNEL, 3], [to, 3 * B]]),
                                  view(y, HALF0 + (C + 5) * B, [[COLS, HALVES], [C * B, 3], [1, 3 * B]]),
                                  view(q, q0 + 5 * B, [[half, HALVES], [0, 3], [1, 3 * B]]), ALU.mult)
                dve.tensor_tensor(view(z, h + CROSS, [[TERMS, HALVES], [4 * CHANNEL, 2], [to, 4 * B]]),
                                  view(y, HALF0 + 4 * C * B, [[COLS, HALVES], [0, 2], [1, 4 * B]]),
                                  view(q, q0 + 4 * B, [[half, HALVES], [4 * B, 2], [1, 4 * B]]),
                                  ALU.mult).then_inc(terms_ready, 1)

            def low_f(i, r):
                wait(dve, f_hi_ready, 2, i, r + 1)
                dve.tensor_tensor(f_lo[:, :, r * P:(r + 1) * P],
                                  down[:, 0, :].rearrange("p (c n) -> p c n", c=HALVES),
                                  f_hi[:, :, r * P:(r + 1) * P], ALU.subtract).then_inc(f_lo_ready, 1)

            def hidden_units(i, t):
                m = chunk_size(t)
                wait(dve, gate_act_ready, CHUNKS, i, t + 1)
                wait_place(dve, h_lo_ready, CHUNKS, i, t - 1)
                dve.scalar_tensor_tensor(out=hidden[0:m, t % 2, :], in0=gate_up[t % 2][0:m, 1, :],
                                         scalar=su_sb[0:m, t:t + 1], in1=gate_act[0:m, t % 2, :],
                                         op0=ALU.mult, op1=ALU.mult).then_inc(hidden_ready, 1)

            def scale_out(i):
                wait(dve, chunk_down, CHUNKS, i, CHUNKS)
                for r in range(2):
                    wait_place(dve, out_ready, 2, i, r - 1)
                    dve.tensor_tensor(ffn_out[:, r, :], down[:, r, :], sd_sb[:, :],
                                      ALU.mult).then_inc(out_scaled, 1)

            def step(i, attention, ffn):
                if attention:
                    norm_q(i, 0)
                if ffn:
                    add_attention(i - 1, 1)
                    norm_f(i - 1, 1)
                    low_f(i - 1, 0)
                if attention:
                    norm_q(i, 1)
                    multiply_terms(i, 0)
                if ffn:
                    low_f(i - 1, 1)
                if attention:
                    multiply_terms(i, 1)
                if ffn:
                    hidden_units(i - 1, 0)
                    hidden_units(i - 1, 1)
                if attention:
                    multiply_terms(i, 2)
                if ffn:
                    hidden_units(i - 1, 2)
                    hidden_units(i - 1, 3)
                    hidden_units(i - 1, 4)
                if attention:
                    multiply_terms(i, 3)
                if ffn:
                    hidden_units(i - 1, 5)
                if attention:
                    add_attention(i, 0)
                if ffn:
                    scale_out(i - 1)
                if attention:
                    norm_f(i, 0)

            dve.wait_ge(x0_loaded, 16)
            variances_q(range(0, 2), 1)
            dve.wait_ge(q_rstd, 1)
            step(0, True, False)
            dve.wait_ge(x_loaded, 16)
            variances_q(range(2, TILES), 2)
            dve.wait_ge(q_rstd, 2)
            with dve.Fori(1, BLOCKS) as i:
                step(i, True, True)
            step(BLOCKS, False, True)

        @block.tensor
        def _(pe):
            def transpose_rows(rows, r, done):
                for c in range(HALVES):
                    last = nc.tensor.transpose(down[:, 0, c * P:(c + 1) * P], rows[:, r, c * P:(c + 1) * P],
                                               ident[:, :])
                last.then_inc(done, 1)

            def turn_q(i, r, ffn):
                wait(pe, q_normed, 2, i, r + 1)
                if r == 0:
                    wait(pe, out_scaled, 2, i, -2)
                elif ffn:
                    wait(pe, f_lo_ready, 2, i, 0)
                else:
                    wait(pe, q_ready, 2, i, 1)
                transpose_rows(q_rows, r, q_turned)

            def turn_f(i, r, attention):
                wait(pe, f_normed, 2, i, r + 1)
                if r == 1:
                    wait(pe, f_lo_ready, 2, i, 1)
                elif attention:
                    wait(pe, q_ready, 2, i, 3)
                else:
                    wait(pe, out_scaled, 2, i, 0)
                transpose_rows(f_rows, r, f_turned)

            def convolve(i, s):
                wait(pe, products_ready, BLOCK_HEADS, i, s + 1)
                wait(pe, toeplitz_loaded[s], 16, i, 16)
                wait(pe, terms_ready, BLOCK_HEADS, i, s - 1)
                y = conv[s % 2]
                halves = [products[:, bass.ds(i * BLOCK_HEADS + s, 1), c * COLS:(c + 1) * COLS]
                          .rearrange("p h n -> p (h n)") for c in range(HALVES)]
                within, across = toeplitz[:, s, 0:P], toeplitz[:, s, P:L]
                nc.tensor.matmul(y[:, HALF0:BANK], within, halves[0], start=True, stop=True)
                nc.tensor.matmul(y[:, BANK:BANK + COLS], within, halves[1], start=True, stop=False)
                nc.tensor.matmul(y[:, BANK:BANK + COLS], across, halves[0], start=False,
                                 stop=True).then_inc(conv_done, 1)

            def sum_terms(i, r):
                wait(pe, terms_ready, BLOCK_HEADS, i, 2 * r + 2)
                wait(pe, x1_steps, 8, i, 4 * r - 3)
                z = terms[:, r, :]
                for c in range(HALVES):
                    for slot in range(C):
                        cols = view(z, c * TERMS + SLOT_AT[slot], [[1, P]])
                        last = nc.tensor.matmul(sums[:, c * P:(c + 1) * P], cols, ident[:, :],
                                                is_transpose=True, start=(slot == 0), stop=(slot == C - 1))
                last.then_inc(summed, 1)

            def gates(i, t):
                m = chunk_size(t)
                if t == 0:
                    wait(pe, f_lo_ready, 2, i, 2)
                wait_place(pe, hidden_ready, CHUNKS, i, t - 1)
                for n, w in enumerate((wg, wu)):
                    for c in range(HALVES):
                        for part in (f_hi, f_lo):
                            last = nc.tensor.matmul(gate_up[t % 2][0:m, n, :], w[:, c, t * P:t * P + m],
                                                    part[:, c, :], start=(c == 0 and part is f_hi),
                                                    stop=(c == HALVES - 1 and part is f_lo))
                last.then_inc(gate_up_done, 1)

            def downs(i, t, attention):
                m = chunk_size(t)
                wait(pe, h_lo_ready, CHUNKS, i, t + 1)
                if t == 0 and attention:
                    wait(pe, q_ready, 2, i, 4)
                for r in range(2):
                    for part in (h_hi, h_lo):
                        last = nc.tensor.matmul(down[:, r, :], part[0:m, t % 3, r * P:(r + 1) * P], wd[0:m, t, :],
                                                start=(t == 0 and r == 0 and part is h_hi),
                                                stop=(t == CHUNKS - 1 and part is h_lo), skip_group_check=True)
                last.then_inc(chunk_down, 1)

            def step(i, attention, ffn):
                if ffn:
                    sum_terms(i - 1, 1)
                if attention:
                    turn_q(i, 0, ffn)
                    convolve(i, 0)
                if ffn:
                    turn_f(i - 1, 0, attention)
                if attention:
                    convolve(i, 1)
                if ffn:
                    turn_f(i - 1, 1, attention)
                    gates(i - 1, 0)
                if attention:
                    turn_q(i, 1, ffn)
                if ffn:
                    gates(i - 1, 1)
                if attention:
                    convolve(i, 2)
                if ffn:
                    gates(i - 1, 2)
                    downs(i - 1, 0, attention)
                    gates(i - 1, 3)
                    downs(i - 1, 1, attention)
                    gates(i - 1, 4)
                if attention:
                    convolve(i, 3)
                if ffn:
                    downs(i - 1, 2, attention)
                    gates(i - 1, 5)
                    downs(i - 1, 3, attention)
                if attention:
                    sum_terms(i, 0)
                if ffn:
                    downs(i - 1, 4, attention)
                    downs(i - 1, 5, attention)

            pe.wait_ge(ident_ready, 1)
            step(0, True, False)
            pe.wait_ge(w_ready, 1)
            with pe.Fori(1, BLOCKS) as i:
                step(i, True, True)
            step(BLOCKS, False, True)


def kernel(x, ctx_2048, L0_xattn_ssm_kernel, L0_xattn_D, L0_ffn_wq_gate, L0_ffn_s_gate, L0_ffn_wq_up,
           L0_ffn_s_up, L0_ffn_wq_down, L0_ffn_s_down):
    import numpy as np
    import concourse.bacc as bacc
    from concourse.bass_utils import run_bass_kernel_spmd

    rows = np.asarray(x).reshape(B, TILES, TILE_HEADS, C, L).transpose(1, 3, 0, 2, 4).reshape(TILES * P, L)
    k = np.asarray(ctx_2048).reshape(B, H, C, HALVES, P)[..., ::-1].transpose(4, 1, 3, 2, 0)
    k = np.concatenate([k, k[:, :, :, :4]], axis=3).reshape(P, H, HALVES, EXT * B)

    def columns(s):
        padded = np.zeros(CHUNKS * P, np.asarray(s).dtype)
        padded[:HID] = np.asarray(s)
        return padded.reshape(CHUNKS, P).T

    arrays = {
        "x": rows,
        "ctx_ext": k,
        "taps": np.asarray(L0_xattn_ssm_kernel),
        "skip": np.asarray(L0_xattn_D).reshape(H, 1),
        "wg_t": np.asarray(L0_ffn_wq_gate).T,
        "s_gate": columns(L0_ffn_s_gate),
        "wu_t": np.asarray(L0_ffn_wq_up).T,
        "s_up": columns(L0_ffn_s_up),
        "wd_t": np.asarray(L0_ffn_wq_down).T,
        "s_down": np.asarray(L0_ffn_s_down),
    }
    arrays = {name: np.ascontiguousarray(a) for name, a in arrays.items()}

    nc = bacc.Bacc("TRN2", target_bir_lowering=False, num_devices=1)
    args = [nc.dram_tensor(name, a.shape, mybir.dt.from_np(a.dtype), kind="ExternalInput").ap()
            for name, a in arrays.items()]
    taps_pad = nc.dram_tensor("taps_pad", (H, P + L), F32).ap()
    out = nc.dram_tensor("out", (H * B * C, L), F32, kind="ExternalOutput").ap()
    build(nc, *args, taps_pad, out)
    got = run_bass_kernel_spmd(nc, [arrays], core_ids=[0]).results[0]["out"]
    return np.asarray(got).reshape(TILES, C, B, TILE_HEADS, L).transpose(2, 0, 3, 1, 4).reshape(B, H * C, L)
```

```python
from contextlib import ExitStack

import concourse.bass as bass
from concourse import mybir

F32 = mybir.dt.float32
F32R = mybir.dt.float32r
F16 = mybir.dt.float16
I32 = mybir.dt.int32
ALU = mybir.AluOpType
ACT = mybir.ActivationFunctionType

P = 128
B, H, C, L = 8, 16, 8, 256
HID = 704
ZERO_POINT = 128.0
EPS = 1e-5

HALVES = L // P
EXT = C + C // 2
PAIRS = C * (C // 2) + C // 2
COLS = B * PAIRS
TILE_HEADS = P // (B * C)
BLOCK_HEADS = 2 * TILE_HEADS
TILES = H // TILE_HEADS
BLOCKS = H // BLOCK_HEADS
ROWS = 2 * P
CHUNKS = -(-HID // P)

CHANNEL = B * TILE_HEADS
SPARE = 3 * CHANNEL
BACK = 4 * P + SPARE
CROSS = BACK + 3 * (P + SPARE)
TERMS = CROSS + P
SLOT_AT = [0, P, 2 * P, 3 * P, BACK, BACK + P + SPARE, BACK + 2 * (P + SPARE), CROSS]


def view(ap, offset, dims):
    return bass.AP(ap.tensor, ap.offset + offset, [list(ap.ap[0])] + [list(d) for d in dims])


def chunk_size(t):
    return min(P, HID - t * P)


def build(nc, x, ctx_ext, taps, skip, wg_t, s_gate, wu_t, s_up, wd_t, s_down, taps_pad, out):
    with ExitStack() as ctx:
        def sb(name, shape, dt=F32):
            return ctx.enter_context(nc.sbuf_tensor(name, shape, dt))

        def sem(name):
            return ctx.enter_context(nc.semaphore(name))

        x_sb = sb("x_sb", [P, TILES, L])
        k_ext = sb("k_ext", [P, H, HALVES, EXT * B])
        products = sb("products", [P, H, HALVES * COLS])
        toeplitz = sb("toeplitz", [P, BLOCK_HEADS, L])
        taps_sb = sb("taps_sb", [H, P + L])
        skip_sb = sb("skip_sb", [H, 1])
        ident = sb("ident", [P, P])
        q_rows = sb("q_rows", [P, 2, L])
        q_ext = sb("q_ext", [P, 2, TILE_HEADS * HALVES * EXT * B])
        terms = sb("terms", [P, 2, HALVES * TERMS])
        ident16 = sb("ident16", [P, P], F16)
        f_rows = sb("f_rows", [P, 2, L])
        f_row_parts = sb("f_row_parts", [P, 2, 2, L], F16)
        f_parts = sb("f_parts", [P, 2, HALVES, ROWS], F16)
        stats_q = sb("stats_q", [P, TILES, 6])
        moments_q = sb("moments_q", [P, TILES, 2])
        variance_q = sb("variance_q", [P, TILES])
        rstd_q = sb("rstd_q", [P, TILES])
        stats_f = sb("stats_f", [P, 2, 6])
        moments_f = sb("moments_f", [P, 2, 2])
        variance_f = sb("variance_f", [P, 2])
        rstd_f = sb("rstd_f", [P, 2])
        minus_half = sb("minus_half", [P, TILES])
        wg_int = sb("wg_int", [P, HALVES, HID], I32)
        wu_int = sb("wu_int", [P, HALVES, HID], I32)
        wd_int = sb("wd_int", [P, CHUNKS, L], I32)
        wg = sb("wg", [P, HALVES, HID], F16)
        wu = sb("wu", [P, HALVES, HID], F16)
        wd = sb("wd", [P, CHUNKS, L], F32R)
        sg_sb = sb("sg_sb", [P, CHUNKS])
        su_sb = sb("su_sb", [P, CHUNKS])
        sd_sb = sb("sd_sb", [P, L])
        gate_act = sb("gate_act", [P, 2, ROWS])
        hidden = sb("hidden", [P, 2, ROWS])
        h_hi = sb("h_hi", [P, 3, ROWS], F32R)
        h_lo = sb("h_lo", [P, 3, ROWS], F32R)
        ffn_out = sb("ffn_out", [P, 2, L])

        BANK = 512
        conv = [ctx.enter_context(nc.psum_tensor(f"conv{n}", [P, 2 * BANK], F32)) for n in range(2)]
        HALF0 = BANK - COLS
        turn = ctx.enter_context(nc.psum_tensor("turn", [P, BANK], F32))
        turn16 = turn[:, :].bitcast(F16).rearrange("p (n c l) -> p n c l", n=4, c=HALVES)[:, 0:2]
        gate_up = [ctx.enter_context(nc.psum_tensor(f"gate_up{n}", [P, 2, ROWS], F32)) for n in range(2)]
        down = ctx.enter_context(nc.psum_tensor("down", [P, 2, L], F32))

        taps_loaded = sem("taps_loaded")
        taps_zeroed = sem("taps_zeroed")
        taps_ready = sem("taps_ready")
        taps_stored = sem("taps_stored")
        toeplitz_loaded = [sem(f"toeplitz_loaded{s}") for s in range(BLOCK_HEADS)]
        x0_loaded, x_loaded = sem("x0_loaded"), sem("x_loaded")
        k0_loaded, k_loaded = sem("k0_loaded"), sem("k_loaded")
        w_loaded = sem("w_loaded")
        w_ready = sem("w_ready")
        ident_zeroed, ident_ready = sem("ident_zeroed"), sem("ident_ready")
        products_ready = sem("products_ready")
        conv_done = sem("conv_done")
        half_ready = sem("half_ready")
        q_stats = sem("q_stats")
        q_moments = sem("q_moments")
        q_variance = sem("q_variance")
        q_rstd = sem("q_rstd")
        q_normed = sem("q_normed")
        q_turned = sem("q_turned")
        q_ready = sem("q_ready")
        terms_ready = sem("terms_ready")
        summed = sem("summed")
        x1_steps = sem("x1_steps")
        f_rstd = sem("f_rstd")
        f_steps = sem("f_steps")
        f_normed = sem("f_normed")
        f_turned = sem("f_turned")
        f_ready = sem("f_ready")
        gate_up_done = sem("gate_up_done")
        gate_act_ready = sem("gate_act_ready")
        hidden_ready = sem("hidden_ready")
        h_hi_ready = sem("h_hi_ready")
        h_lo_ready = sem("h_lo_ready")
        chunk_down = sem("chunk_down")
        waited = sem("waited")
        out_scaled = sem("out_scaled")
        out_ready = sem("out_ready")
        out_stored = sem("out_stored")

        credited = (chunk_down, hidden_ready, h_lo_ready, out_ready, out_scaled)

        def wait(eng, semaphore, per_block, block, offset):
            credit = 1 if semaphore in credited else 0
            if not isinstance(block, int) or per_block * block + offset > 0:
                eng.wait_ge(semaphore, block * per_block + (offset + credit))

        def wait_place(eng, semaphore, per_block, block, offset):
            wait(eng, semaphore, per_block, block, offset if isinstance(block, int) else max(offset, 0))

        block = ctx.enter_context(nc.Block())

        @block.sync
        def _(sp):
            def load_toeplitz(i, s):
                src = bass.AP(taps_pad.tensor, (i * BLOCK_HEADS + s) * (P + L) + 1, [[1, P], [1, L]])
                sp.dma_start(toeplitz[:, s, :], src).then_inc(toeplitz_loaded[s], 16)

            def store(i, r):
                wait(sp, out_ready, 2, i, r + 1)
                sp.dma_start(out_at(i, r), x_at(i, r)).then_inc(out_stored, 16)

            def out_at(i, r):
                return out[bass.ds((i * 2 + r) * P, P), :]

            def x_at(i, r):
                return x_sb[:, bass.ds(i * 2 + r, 1), :]

            sp.dma_start(taps_sb[:, P:], taps).then_inc(taps_loaded, 16)
            sp.dma_start(skip_sb[:, :], skip).then_inc(taps_loaded, 16)
            sp.dma_start(k_ext[:, 0:BLOCK_HEADS], ctx_ext[:, 0:BLOCK_HEADS]).then_inc(k0_loaded, 16)
            sp.wait_ge(taps_ready, 1)
            sp.dma_start(taps_pad, taps_sb[:, :]).then_inc(taps_stored, 16)
            sp.wait_ge(taps_stored, 16)
            for s in range(BLOCK_HEADS):
                load_toeplitz(0, s)
            sp.dma_start(k_ext[:, BLOCK_HEADS:], ctx_ext[:, BLOCK_HEADS:]).then_inc(k_loaded, 16)
            full = (CHUNKS - 1) * P
            sp.dma_start(wg_int[:, :, :], wg_t.rearrange("(c p) n -> p c n", p=P)).then_inc(w_loaded, 16)
            sp.dma_start(wu_int[:, :, :], wu_t.rearrange("(c p) n -> p c n", p=P)).then_inc(w_loaded, 16)
            sp.dma_start(wd_int[:, 0:CHUNKS - 1, :],
                         wd_t[0:full, :].rearrange("(t p) n -> p t n", p=P)).then_inc(w_loaded, 16)
            sp.dma_start(wd_int[0:HID - full, CHUNKS - 1, :], wd_t[full:HID, :]).then_inc(w_loaded, 16)
            sp.dma_start(sg_sb[:, :], s_gate).then_inc(w_loaded, 16)
            sp.dma_start(su_sb[:, :], s_up).then_inc(w_loaded, 16)
            sp.dma_start(sd_sb[:, :], s_down.partition_broadcast(P)).then_inc(w_loaded, 16)
            def reload(i):
                for s in range(BLOCK_HEADS):
                    wait(sp, conv_done, BLOCK_HEADS, i, s + 1)
                    load_toeplitz(i + 1, s)

            reload(0)
            with sp.Fori(1, BLOCKS - 1) as i:
                reload(i)
                store(i - 1, 0)
                store(i - 1, 1)
            for i in range(BLOCKS - 2, BLOCKS):
                store(i, 0)
                store(i, 1)
            sp.wait_ge(out_stored, 16 * TILES)

        @block.gpsimd
        def _(pool):
            for semaphore in credited:
                pool.sem_inc(semaphore, 1)
            nc.gpsimd.memset(minus_half[:, :], -0.5).then_inc(half_ready, 1)
            nc.gpsimd.memset(ident[:, :], 0.0).then_inc(ident_zeroed, 1)
            pool.wait_ge(half_ready, 1)
            pool.wait_ge(ident_zeroed, 1)
            nc.gpsimd.affine_select(out=ident[:, :], in_=ident[:, :], compare_op=ALU.not_equal, fill=1.0,
                                    base=0, pattern=[[-1, P]], channel_multiplier=1).then_inc(ident_ready, 1)
            pool.wait_ge(ident_ready, 1)
            nc.gpsimd.tensor_copy(ident16[:, :], ident[:, :]).then_inc(ident_ready, 1)

            def multiply_pairs(n):
                k = k_ext[:, bass.ds(n, 1)]
                o = products[:, bass.ds(n, 1)]
                nc.gpsimd.tensor_tensor(
                    view(o, 0, [[COLS, HALVES], [C * B, 4], [1, C * B]]),
                    view(k, 0, [[EXT * B, HALVES], [0, 4], [1, C * B]]),
                    view(k, 0, [[EXT * B, HALVES], [B, 4], [1, C * B]]), ALU.mult)
                nc.gpsimd.tensor_tensor(
                    view(o, 4 * C * B, [[COLS, HALVES], [1, 4 * B]]),
                    view(k, 0, [[EXT * B, HALVES], [1, 4 * B]]),
                    view(k, 4 * B, [[EXT * B, HALVES], [1, 4 * B]]), ALU.mult).then_inc(products_ready, 1)

            def root(base, power, result, done):
                nc.gpsimd.tensor_tensor(result, base, power, ALU.pow).then_inc(done, 1)

            def root_q(tiles, count):
                pool.wait_ge(q_variance, count)
                root(variance_q[:, tiles], minus_half[:, tiles], rstd_q[:, tiles], q_rstd)

            def root_f(i, r):
                wait(pool, x1_steps, 8, i, 4 * r + 4)
                wait(pool, f_normed, 2, i, r - 1)
                root(variance_f[:, r:r + 1], minus_half[:, 0:1], rstd_f[:, r:r + 1], f_rstd)

            def low_hidden(i, t):
                m = chunk_size(t)
                wait(pool, h_hi_ready, CHUNKS, i, t + 1)
                wait_place(pool, chunk_down, CHUNKS, i, t - 2)
                nc.gpsimd.tensor_tensor(h_lo[0:m, t % 3, :], hidden[0:m, t % 2, :], h_hi[0:m, t % 3, :],
                                        ALU.subtract).then_inc(h_lo_ready, 1)

            def add_ffn(i, r):
                x1 = x_sb[:, bass.ds(i * 2 + r, 1), :]
                wait(pool, out_scaled, 2, i, r + 1)
                nc.gpsimd.tensor_tensor(x1, x1, ffn_out[:, r:r + 1, :], ALU.add).then_inc(out_ready, 1)

            def step(i, ffn, current, following):
                n = BLOCK_HEADS * i + BLOCK_HEADS
                if following:
                    multiply_pairs(n)
                if ffn:
                    low_hidden(i - 1, 0)
                    low_hidden(i - 1, 1)
                if following:
                    multiply_pairs(n + 1)
                if ffn:
                    low_hidden(i - 1, 2)
                    low_hidden(i - 1, 3)
                    low_hidden(i - 1, 4)
                if following:
                    multiply_pairs(n + 2)
                if current:
                    root_f(i, 0)
                if ffn:
                    low_hidden(i - 1, 5)
                if following:
                    multiply_pairs(n + 3)
                if current:
                    root_f(i, 1)
                if ffn:
                    add_ffn(i - 1, 0)
                    add_ffn(i - 1, 1)

            pool.wait_ge(k0_loaded, 16)
            multiply_pairs(0)
            root_q(slice(0, 2), 1)
            multiply_pairs(1)
            multiply_pairs(2)
            multiply_pairs(3)
            root_q(slice(2, TILES), 2)
            pool.wait_ge(k_loaded, 16)
            step(0, False, True, True)
            with pool.Fori(1, BLOCKS - 1) as i:
                step(i, True, True, True)
            step(BLOCKS - 1, True, True, False)
            step(BLOCKS, True, False, False)

        @block.scalar
        def _(act):
            def evict_q(i, r):
                wait(act, q_turned, 2, i, r + 1)
                wait(act, terms_ready, BLOCK_HEADS, i, 2 * r + 2 - BLOCK_HEADS)
                o, src = q_ext[:, r, :], turn[:, :]
                half, head = EXT * B, HALVES * EXT * B
                nc.scalar.activation(
                    view(o, 0, [[head, TILE_HEADS], [half, HALVES], [1, C * B]]),
                    view(src, 0, [[1, TILE_HEADS], [P, HALVES], [TILE_HEADS, C * B]]), ACT.Copy)
                nc.scalar.activation(
                    view(o, C * B, [[head, TILE_HEADS], [half, HALVES], [1, 4 * B]]),
                    view(src, 0, [[1, TILE_HEADS], [P, HALVES], [TILE_HEADS, 4 * B]]),
                    ACT.Copy).then_inc(q_ready, 1)

            def evict_f(i, r):
                wait(act, f_turned, 2, i, r + 1)
                nc.scalar.activation(f_parts[:, :, :, r * P:(r + 1) * P], turn16, ACT.Copy).then_inc(f_ready, 1)

            def gate(i, t):
                m = chunk_size(t)
                wait(act, gate_up_done, CHUNKS, i, t + 1)
                wait_place(act, hidden_ready, CHUNKS, i, t - 1)
                nc.scalar.activation(gate_act[0:m, t % 2, :], gate_up[t % 2][0:m, 0, :], ACT.Silu,
                                     scale=sg_sb[0:m, t:t + 1]).then_inc(gate_act_ready, 1)

            def hidden_high(i, t):
                m = chunk_size(t)
                wait(act, hidden_ready, CHUNKS, i, t + 1)
                wait_place(act, chunk_down, CHUNKS, i, t - 2)
                nc.scalar.activation(h_hi[0:m, t % 3, :], hidden[0:m, t % 2, :], ACT.Copy).then_inc(h_hi_ready, 1)

            def convert_weights():
                act.wait_ge(w_loaded, 7 * 16)
                nc.scalar.activation(wg[:, :, :], wg_int[:, :, :], ACT.Copy, bias=-ZERO_POINT)
                nc.scalar.activation(wu[:, :, :], wu_int[:, :, :], ACT.Copy, bias=-ZERO_POINT)
                nc.scalar.activation(wd[:, 0:CHUNKS - 1, :], wd_int[:, 0:CHUNKS - 1, :], ACT.Copy, bias=-ZERO_POINT)
                m = chunk_size(CHUNKS - 1)
                nc.scalar.activation(wd[0:m, CHUNKS - 1, :], wd_int[0:m, CHUNKS - 1, :], ACT.Copy,
                                     bias=-ZERO_POINT).then_inc(w_ready, 1)

            def step(i, ffn, current, following):
                if ffn:
                    gate(i - 1, 0)
                if current:
                    evict_q(i, 1)
                if ffn:
                    gate(i - 1, 1)
                    hidden_high(i - 1, 0)
                    hidden_high(i - 1, 1)
                    for t in range(2, CHUNKS):
                        gate(i - 1, t)
                        hidden_high(i - 1, t)
                if following:
                    evict_q(i + 1, 0)
                if current:
                    evict_f(i, 0)
                    evict_f(i, 1)

            act.dma_start(x_sb[:, 0:2, :], x[0:ROWS, :].rearrange("(t p) l -> p t l", p=P)).then_inc(x0_loaded, 16)
            act.dma_start(x_sb[:, 2:TILES, :], x[ROWS:, :].rearrange("(t p) l -> p t l", p=P)).then_inc(x_loaded, 16)
            nc.scalar.preload_act_table(ACT.Silu)
            evict_q(0, 0)
            evict_q(0, 1)
            convert_weights()
            evict_q(1, 0)
            evict_f(0, 0)
            evict_f(0, 1)
            with act.Fori(1, BLOCKS - 1) as i:
                step(i, True, True, True)
            step(BLOCKS - 1, True, True, False)
            step(BLOCKS, True, False, False)

        @block.vector
        def _(dve):
            dve.memset(taps_sb[:, 0:P], 0.0).then_inc(taps_zeroed, 1)
            dve.wait_ge(taps_loaded, 32)
            dve.wait_ge(taps_zeroed, 1)
            dve.tensor_tensor(taps_sb[:, P:P + 1], taps_sb[:, P:P + 1], skip_sb[:, :], ALU.add).then_inc(taps_ready, 1)

            def tile_of(i, r):
                return x_sb[:, bass.ds(i * 2 + r, 1), :].rearrange("p t l -> p (t l)")

            def variances_q(tiles, count):
                for t in tiles:
                    last = dve.bn_stats(stats_q[:, t, :], x_sb[:, t, :])
                last.then_inc(q_stats, 1)
                dve.wait_ge(q_stats, count)
                for t in tiles:
                    last = dve.bn_aggr(moments_q[:, t, :], stats_q[:, t, :])
                last.then_inc(q_moments, 1)
                dve.wait_ge(q_moments, count)
                dve.tensor_scalar(variance_q[:, tiles[0]:tiles[-1] + 1],
                                  view(moments_q[:, tiles[0], :], 1, [[2, len(tiles)]]), EPS, None,
                                  ALU.add).then_inc(q_variance, 1)

            def norm_q(i, r):
                tile = bass.ds(i * 2 + r, 1)
                wait(dve, q_turned, 2, i, r - 1)
                dve.tensor_scalar(q_rows[:, r, :], tile_of(i, r),
                                  moments_q[:, tile, 0:1].rearrange("p t c -> p (t c)"), rstd_q[:, tile],
                                  ALU.subtract, ALU.mult).then_inc(q_normed, 1)

            def wait_apart(semaphore, per_block, i, offset):
                wait(dve, semaphore, per_block, i, offset)
                dve.sem_inc(waited, 1)

            def add_attention(i, r):
                x1 = tile_of(i, r)
                wait(dve, summed, 2, i, r + 1)
                dve.tensor_tensor(x1, x1, turn[:, 0:L], ALU.add).then_inc(x1_steps, 1)
                wait_apart(x1_steps, 8, i, 4 * r + 1)
                dve.bn_stats(stats_f[:, r, :], x1).then_inc(x1_steps, 1)
                wait_apart(x1_steps, 8, i, 4 * r + 2)
                dve.bn_aggr(moments_f[:, r, :], stats_f[:, r, :]).then_inc(x1_steps, 1)
                wait(dve, x1_steps, 8, i, 4 * r + 3)
                dve.tensor_scalar(variance_f[:, r:r + 1], moments_f[:, r, 1:2], EPS, None,
                                  ALU.add).then_inc(x1_steps, 1)

            def norm_f(i, r):
                wait(dve, f_rstd, 2, i, r + 1)
                dve.tensor_scalar(f_rows[:, r, :], tile_of(i, r), moments_f[:, r, 0:1], rstd_f[:, r:r + 1],
                                  ALU.subtract, ALU.mult).then_inc(f_steps, 1)
                wait(dve, f_steps, 4, i, 2 * r + 1)
                wait(dve, f_turned, 2, i, r - 1)
                dve.tensor_copy(f_row_parts[:, r, 0, :], f_rows[:, r, :]).then_inc(f_steps, 1)
                wait(dve, f_steps, 4, i, 2 * r + 2)
                dve.tensor_tensor(f_row_parts[:, r, 1, :], f_rows[:, r, :], f_row_parts[:, r, 0, :],
                                  ALU.subtract).then_inc(f_normed, 1)

            def multiply_terms(i, s):
                r, h = s // TILE_HEADS, s % TILE_HEADS
                wait(dve, conv_done, BLOCK_HEADS, i, s + 1)
                if h == 0:
                    wait(dve, q_ready, 2, i, r + 1)
                    wait(dve, summed, 2, i, r - 1)
                y = conv[s % 2][:, :]
                q = q_ext[:, r, :]
                z = terms[:, r, :]
                half = EXT * B
                q0 = h * HALVES * half
                to = TILE_HEADS
                dve.tensor_tensor(view(z, h, [[TERMS, HALVES], [P, 4], [to, C * B]]),
                                  view(y, HALF0, [[COLS, HALVES], [C * B, 4], [1, C * B]]),
                                  view(q, q0, [[half, HALVES], [B, 4], [1, C * B]]), ALU.mult)
                dve.tensor_tensor(view(z, h + BACK + CHANNEL,
                                       [[TERMS, HALVES], [P + SPARE + CHANNEL, 3], [to, C * B]]),
                                  view(y, HALF0 + C * B, [[COLS, HALVES], [C * B, 3], [1, C * B]]),
                                  view(q, q0, [[half, HALVES], [0, 3], [1, C * B]]), ALU.mult)
                dve.tensor_tensor(view(z, h + BACK - 2 * CHANNEL,
                                       [[TERMS, HALVES], [P + SPARE + CHANNEL, 3], [to, 3 * B]]),
                                  view(y, HALF0 + (C + 5) * B, [[COLS, HALVES], [C * B, 3], [1, 3 * B]]),
                                  view(q, q0 + 5 * B, [[half, HALVES], [0, 3], [1, 3 * B]]), ALU.mult)
                dve.tensor_tensor(view(z, h + CROSS, [[TERMS, HALVES], [4 * CHANNEL, 2], [to, 4 * B]]),
                                  view(y, HALF0 + 4 * C * B, [[COLS, HALVES], [0, 2], [1, 4 * B]]),
                                  view(q, q0 + 4 * B, [[half, HALVES], [4 * B, 2], [1, 4 * B]]),
                                  ALU.mult).then_inc(terms_ready, 1)

            def hidden_units(i, t):
                m = chunk_size(t)
                wait(dve, gate_act_ready, CHUNKS, i, t + 1)
                wait_place(dve, h_lo_ready, CHUNKS, i, t - 1)
                dve.scalar_tensor_tensor(out=hidden[0:m, t % 2, :], in0=gate_up[t % 2][0:m, 1, :],
                                         scalar=su_sb[0:m, t:t + 1], in1=gate_act[0:m, t % 2, :],
                                         op0=ALU.mult, op1=ALU.mult).then_inc(hidden_ready, 1)

            def scale_out(i):
                wait(dve, chunk_down, CHUNKS, i, CHUNKS)
                for r in range(2):
                    wait_place(dve, out_ready, 2, i, r - 1)
                    dve.tensor_tensor(ffn_out[:, r, :], down[:, r, :], sd_sb[:, :],
                                      ALU.mult).then_inc(out_scaled, 1)

            def step(i, ffn, current, following):
                if ffn:
                    hidden_units(i - 1, 0)
                    hidden_units(i - 1, 1)
                if current:
                    multiply_terms(i, 2)
                if ffn:
                    hidden_units(i - 1, 2)
                    hidden_units(i - 1, 3)
                    hidden_units(i - 1, 4)
                if current:
                    multiply_terms(i, 3)
                    add_attention(i, 0)
                if ffn:
                    hidden_units(i - 1, 5)
                if following:
                    norm_q(i + 1, 0)
                if current:
                    norm_f(i, 0)
                if following:
                    norm_q(i + 1, 1)
                if current:
                    add_attention(i, 1)
                    norm_f(i, 1)
                if following:
                    multiply_terms(i + 1, 0)
                    multiply_terms(i + 1, 1)
                if ffn:
                    scale_out(i - 1)

            dve.wait_ge(x0_loaded, 16)
            variances_q(range(0, 2), 1)
            dve.wait_ge(q_rstd, 1)
            norm_q(0, 0)
            norm_q(0, 1)
            dve.wait_ge(x_loaded, 16)
            variances_q(range(2, TILES), 2)
            multiply_terms(0, 0)
            multiply_terms(0, 1)
            dve.wait_ge(q_rstd, 2)
            step(0, False, True, True)
            with dve.Fori(1, BLOCKS - 1) as i:
                step(i, True, True, True)
            step(BLOCKS - 1, True, True, False)
            step(BLOCKS, True, False, False)

        @block.tensor
        def _(pe):
            def turn_q(i, r):
                wait(pe, q_normed, 2, i, r + 1)
                if r == 0:
                    wait(pe, x1_steps, 8, i, -3)
                elif isinstance(i, int) and i == 0:
                    wait(pe, q_ready, 2, i, 1)
                else:
                    wait(pe, f_ready, 2, i, 0)
                for c in range(HALVES):
                    last = nc.tensor.transpose(turn[:, c * P:(c + 1) * P], q_rows[:, r, c * P:(c + 1) * P],
                                               ident[:, :])
                last.then_inc(q_turned, 1)

            def turn_f(i, r, following):
                wait(pe, f_normed, 2, i, r + 1)
                if r == 1:
                    wait(pe, f_ready, 2, i, 1)
                elif following:
                    wait(pe, q_ready, 2, i, 3)
                else:
                    wait(pe, x1_steps, 8, i, 5)
                for part in range(2):
                    for c in range(HALVES):
                        last = nc.tensor.transpose(turn16[:, part, c, :],
                                                   f_row_parts[:, r, part, c * P:(c + 1) * P], ident16[:, :])
                last.then_inc(f_turned, 1)

            def convolve(i, s):
                wait(pe, products_ready, BLOCK_HEADS, i, s + 1)
                wait(pe, toeplitz_loaded[s], 16, i, 16)
                wait(pe, terms_ready, BLOCK_HEADS, i, s - 1)
                y = conv[s % 2]
                halves = [products[:, bass.ds(i * BLOCK_HEADS + s, 1), c * COLS:(c + 1) * COLS]
                          .rearrange("p h n -> p (h n)") for c in range(HALVES)]
                within, across = toeplitz[:, s, 0:P], toeplitz[:, s, P:L]
                nc.tensor.matmul(y[:, HALF0:BANK], within, halves[0], start=True, stop=True)
                nc.tensor.matmul(y[:, BANK:BANK + COLS], within, halves[1], start=True, stop=False)
                nc.tensor.matmul(y[:, BANK:BANK + COLS], across, halves[0], start=False,
                                 stop=True).then_inc(conv_done, 1)

            def sum_terms(i, r):
                wait(pe, terms_ready, BLOCK_HEADS, i, 2 * r + 2)
                if r == 0:
                    wait(pe, q_ready, 2, i, 2)
                else:
                    wait(pe, x1_steps, 8, i, 1)
                z = terms[:, r, :]
                for c in range(HALVES):
                    for slot in range(C):
                        cols = view(z, c * TERMS + SLOT_AT[slot], [[1, P]])
                        last = nc.tensor.matmul(turn[:, c * P:(c + 1) * P], cols, ident[:, :],
                                                is_transpose=True, start=(slot == 0), stop=(slot == C - 1))
                last.then_inc(summed, 1)

            def gates(i, t):
                m = chunk_size(t)
                if t == 0:
                    wait(pe, f_ready, 2, i, 2)
                wait_place(pe, hidden_ready, CHUNKS, i, t - 1)
                for n, w in enumerate((wg, wu)):
                    for c in range(HALVES):
                        for part in range(2):
                            last = nc.tensor.matmul(gate_up[t % 2][0:m, n, :], w[:, c, t * P:t * P + m],
                                                    f_parts[:, part, c, :], start=(c == 0 and part == 0),
                                                    stop=(c == HALVES - 1 and part == 1))
                last.then_inc(gate_up_done, 1)

            def downs(i, t):
                m = chunk_size(t)
                wait(pe, h_lo_ready, CHUNKS, i, t + 1)
                if t == 0:
                    wait_place(pe, out_scaled, 2, i, 0)
                for r in range(2):
                    for part in (h_hi, h_lo):
                        last = nc.tensor.matmul(down[:, r, :], part[0:m, t % 3, r * P:(r + 1) * P], wd[0:m, t, :],
                                                start=(t == 0 and r == 0 and part is h_hi),
                                                stop=(t == CHUNKS - 1 and part is h_lo), skip_group_check=True)
                last.then_inc(chunk_down, 1)

            def step(i, ffn, current, following):
                if ffn:
                    gates(i - 1, 0)
                if current:
                    turn_q(i, 1)
                if ffn:
                    gates(i - 1, 1)
                if current:
                    convolve(i, 2)
                if ffn:
                    gates(i - 1, 2)
                    downs(i - 1, 0)
                    gates(i - 1, 3)
                    downs(i - 1, 1)
                    gates(i - 1, 4)
                if current:
                    convolve(i, 3)
                if ffn:
                    downs(i - 1, 2)
                if current:
                    sum_terms(i, 0)
                if ffn:
                    gates(i - 1, 5)
                    downs(i - 1, 3)
                if current:
                    sum_terms(i, 1)
                if following:
                    convolve(i + 1, 0)
                    turn_q(i + 1, 0)
                    convolve(i + 1, 1)
                if current:
                    turn_f(i, 0, following)
                if ffn:
                    downs(i - 1, 4)
                    downs(i - 1, 5)
                if current:
                    turn_f(i, 1, following)

            pe.wait_ge(ident_ready, 2)
            turn_q(0, 0)
            convolve(0, 0)
            convolve(0, 1)
            step(0, False, True, True)
            pe.wait_ge(w_ready, 1)
            with pe.Fori(1, BLOCKS - 1) as i:
                step(i, True, True, True)
            step(BLOCKS - 1, True, True, False)
            step(BLOCKS, True, False, False)


def kernel(x, ctx_2048, L0_xattn_ssm_kernel, L0_xattn_D, L0_ffn_wq_gate, L0_ffn_s_gate, L0_ffn_wq_up,
           L0_ffn_s_up, L0_ffn_wq_down, L0_ffn_s_down):
    import numpy as np
    import concourse.bacc as bacc
    from concourse.bass_utils import run_bass_kernel_spmd

    rows = np.asarray(x).reshape(B, TILES, TILE_HEADS, C, L).transpose(1, 3, 0, 2, 4).reshape(TILES * P, L)
    k = np.asarray(ctx_2048).reshape(B, H, C, HALVES, P)[..., ::-1].transpose(4, 1, 3, 2, 0)
    k = np.concatenate([k, k[:, :, :, :4]], axis=3).reshape(P, H, HALVES, EXT * B)

    def columns(s):
        padded = np.zeros(CHUNKS * P, np.asarray(s).dtype)
        padded[:HID] = np.asarray(s)
        return padded.reshape(CHUNKS, P).T

    arrays = {
        "x": rows,
        "ctx_ext": k,
        "taps": np.asarray(L0_xattn_ssm_kernel),
        "skip": np.asarray(L0_xattn_D).reshape(H, 1),
        "wg_t": np.asarray(L0_ffn_wq_gate).T,
        "s_gate": columns(L0_ffn_s_gate),
        "wu_t": np.asarray(L0_ffn_wq_up).T,
        "s_up": columns(L0_ffn_s_up),
        "wd_t": np.asarray(L0_ffn_wq_down).T,
        "s_down": np.asarray(L0_ffn_s_down),
    }
    arrays = {name: np.ascontiguousarray(a) for name, a in arrays.items()}

    nc = bacc.Bacc("TRN2", target_bir_lowering=False, num_devices=1)
    args = [nc.dram_tensor(name, a.shape, mybir.dt.from_np(a.dtype), kind="ExternalInput").ap()
            for name, a in arrays.items()]
    taps_pad = nc.dram_tensor("taps_pad", (H, P + L), F32).ap()
    out = nc.dram_tensor("out", (H * B * C, L), F32, kind="ExternalOutput").ap()
    build(nc, *args, taps_pad, out)
    got = run_bass_kernel_spmd(nc, [arrays], core_ids=[0]).results[0]["out"]
    return np.asarray(got).reshape(TILES, C, B, TILE_HEADS, L).transpose(2, 0, 3, 1, 4).reshape(B, H * C, L)
```

```python
from contextlib import ExitStack

import concourse.bass as bass
from concourse import mybir

F32 = mybir.dt.float32
F32R = mybir.dt.float32r
F16 = mybir.dt.float16
I32 = mybir.dt.int32
ALU = mybir.AluOpType
ACT = mybir.ActivationFunctionType

P = 128
B, H, C, L = 8, 16, 8, 256
HID = 704
ZERO_POINT = 128.0
EPS = 1e-5

HALVES = L // P
EXT = C + C // 2
PAIRS = C * (C // 2) + C // 2
COLS = B * PAIRS
TILE_HEADS = P // (B * C)
BLOCK_HEADS = 2 * TILE_HEADS
TILES = H // TILE_HEADS
BLOCKS = H // BLOCK_HEADS
ROWS = 2 * P
CHUNKS = -(-HID // P)
FULL = CHUNKS - 1
TAIL = HID - FULL * P
assert 2 * TAIL == P
FILL_START = 23
FILL = 6

CHANNEL = B * TILE_HEADS
SPARE = 3 * CHANNEL
BACK = 4 * P + SPARE
CROSS = BACK + 3 * (P + SPARE)
TERMS = CROSS + P
SUMMED_SLOTS = [0, 2 * P, BACK, BACK + P + SPARE, BACK + 2 * (P + SPARE), CROSS]


def view(ap, offset, dims):
    return bass.AP(ap.tensor, ap.offset + offset, [list(ap.ap[0])] + [list(d) for d in dims])


def gate_lanes(t):
    return slice(0, P if t < FULL else TAIL)


def up_lanes(t):
    return slice(0, P) if t < FULL else slice(TAIL, P)


def build(nc, x, ctx_ext, taps, skip, wg_t, s_gate, wu_t, s_up, wd_t, s_down, taps_pad, out):
    with ExitStack() as ctx:
        def sb(name, shape, dt=F32):
            return ctx.enter_context(nc.sbuf_tensor(name, shape, dt))

        def sem(name):
            return ctx.enter_context(nc.semaphore(name))

        x_sb = sb("x_sb", [P, TILES, L])
        k_ext = sb("k_ext", [P, H, HALVES, EXT * B])
        products = sb("products", [P, H, HALVES * COLS])
        windows = sb("windows", [P, BLOCK_HEADS, L])
        toeplitz = sb("toeplitz", [P, BLOCK_HEADS, L])
        taps_sb = sb("taps_sb", [H, P + L])
        skip_all = sb("skip_all", [P, H])
        anti = sb("anti", [P, P])
        skip_sb = sb("skip_sb", [H, 1])
        ident = sb("ident", [P, P])
        zeros = sb("zeros", [P, 2 * P], F16)
        q_rows = sb("q_rows", [P, 2, L])
        q_ext = sb("q_ext", [P, 2, TILE_HEADS * HALVES * EXT * B])
        terms = sb("terms", [P, 2, HALVES * TERMS])
        ident16 = sb("ident16", [P, P], F16)
        f_rows = sb("f_rows", [P, 2, L])
        f_row_parts = sb("f_row_parts", [P, 2, 2, L], F16)
        f_parts = sb("f_parts", [P, 2, HALVES, ROWS], F16)
        last_f_parts = sb("last_f_parts", [P, 2, HALVES, ROWS], F16)
        stats_q = sb("stats_q", [P, 2, 6])
        moments_q = sb("moments_q", [P, 2, 2])
        variance_q = sb("variance_q", [P, 2])
        rstd_q = sb("rstd_q", [P, 2])
        stats_f = sb("stats_f", [P, 2, 6])
        moments_f = sb("moments_f", [P, 2, 2])
        variance_f = sb("variance_f", [P, 2])
        rstd_f = sb("rstd_f", [P, 2])
        minus_half = sb("minus_half", [P, 2])
        wg_int = sb("wg_int", [P, HALVES, HID], I32)
        wu_int = sb("wu_int", [P, HALVES, HID], I32)
        wd_int = sb("wd_int", [P, CHUNKS, L], I32)
        wgu = sb("wgu", [P, HALVES, 2 * HID], F16)
        wd = sb("wd", [P, CHUNKS, L], F32R)
        sg_sb = sb("sg_sb", [P, CHUNKS])
        su_sb = sb("su_sb", [P, CHUNKS])
        sd_sb = sb("sd_sb", [P, L])
        gate_act = sb("gate_act", [P, CHUNKS, ROWS])
        hidden = sb("hidden", [P, CHUNKS, ROWS])
        h_hi = sb("h_hi", [P, FULL, ROWS], F32R)
        h_lo = sb("h_lo", [P, FULL, ROWS], F32R)
        h_tail = sb("h_tail", [P, ROWS], F32R)
        ffn_out = sb("ffn_out", [P, 2, L])

        BANK = 512
        conv = [ctx.enter_context(nc.psum_tensor(f"conv{n}", [P, 2 * BANK], F32)) for n in range(2)]
        HALF0 = BANK - COLS
        turn = ctx.enter_context(nc.psum_tensor("turn", [P, BANK], F32))
        turn16 = turn[:, :].bitcast(F16).rearrange("p (n c l) -> p n c l", n=4, c=HALVES)[:, 0:2]
        gate_up = [ctx.enter_context(nc.psum_tensor(f"gate_up{n}", [P, 2, ROWS], F32)) for n in range(2)]
        down = ctx.enter_context(nc.psum_tensor("down", [P, 2, L], F32))

        taps_loaded = sem("taps_loaded")
        taps_ready = sem("taps_ready")
        taps_stored = sem("taps_stored")
        windows_loaded = [sem("window0_loaded"), sem("windows_loaded")]
        skip_loaded = sem("skip_loaded")
        windows_ready = sem("windows_ready")
        toeplitz_loaded = [sem(f"toeplitz_loaded{s}") for s in range(BLOCK_HEADS)]
        x0_loaded, x_loaded = sem("x0_loaded"), sem("x_loaded")
        k_loaded = [sem("k_head0_loaded"), sem("k_block0_loaded"), sem("k_block1_loaded"), sem("k_loaded")]
        w_loaded = [sem("wg_loaded"), sem("wu_loaded"), sem("wd_loaded")]
        w_ready = sem("w_ready")
        zeros_ready = sem("zeros_ready")
        ident_zeroed, ident_ready, anti_ready = sem("ident_zeroed"), sem("ident_ready"), sem("anti_ready")
        first_made = sem("first_made")
        made = sem("made")
        conv_done = sem("conv_done")
        half_ready = sem("half_ready")
        q_stats = sem("q_stats")
        q_moments = sem("q_moments")
        q_variance = sem("q_variance")
        q_rstd = sem("q_rstd")
        q_normed = sem("q_normed")
        q_turned = sem("q_turned")
        q_ready = sem("q_ready")
        terms_ready = sem("terms_ready")
        merged = sem("merged")
        summed = sem("summed")
        x1_steps = sem("x1_steps")
        f_rstd = sem("f_rstd")
        f_steps = sem("f_steps")
        f_normed = sem("f_normed")
        f_turned = sem("f_turned")
        f_ready = sem("f_ready")
        gate_up_done = sem("gate_up_done")
        gate_act_ready = sem("gate_act_ready")
        hidden_ready = sem("hidden_ready")
        h_hi_ready = sem("h_hi_ready")
        h_lo_ready = sem("h_lo_ready")
        last_h_lo_ready = sem("last_h_lo_ready")
        tail_ready = sem("tail_ready")
        chunk_down = sem("chunk_down")
        waited = sem("waited")
        out_scaled = sem("out_scaled")
        out_ready = sem("out_ready")
        out_stored = sem("out_stored")

        credited = (chunk_down, hidden_ready, h_lo_ready, out_ready, out_scaled)

        def wait(eng, semaphore, per_block, block, offset):
            credit = 1 if semaphore in credited else 0
            if not isinstance(block, int) or per_block * block + offset > 0:
                eng.wait_ge(semaphore, block * per_block + (offset + credit))

        def wait_place(eng, semaphore, per_block, block, offset):
            wait(eng, semaphore, per_block, block, offset if isinstance(block, int) else max(offset, 0))

        def multiply_pairs(eng, n, done):
            k = k_ext[:, bass.ds(n, 1)]
            o = products[:, bass.ds(n, 1)]
            eng.tensor_tensor(
                view(o, 0, [[COLS, HALVES], [C * B, 4], [1, C * B]]),
                view(k, 0, [[EXT * B, HALVES], [0, 4], [1, C * B]]),
                view(k, 0, [[EXT * B, HALVES], [B, 4], [1, C * B]]), ALU.mult)
            eng.tensor_tensor(
                view(o, 4 * C * B, [[COLS, HALVES], [1, 4 * B]]),
                view(k, 0, [[EXT * B, HALVES], [1, 4 * B]]),
                view(k, 4 * B, [[EXT * B, HALVES], [1, 4 * B]]), ALU.mult).then_inc(done, 1)

        def is_last(i):
            return isinstance(i, int) and i == BLOCKS - 1

        def high_of(t):
            return h_hi[:, t, :] if t < FULL else h_tail[TAIL:P, :]

        def subtract_high(eng, i, t):
            wait(eng, h_hi_ready, CHUNKS, i, t + 1)
            wait_place(eng, chunk_down, CHUNKS, i, t + 1 - CHUNKS)
            low = h_lo[:, t, :] if t < FULL else h_tail[0:TAIL, :]
            done = tail_ready if t == FULL else last_h_lo_ready if is_last(i) else h_lo_ready
            eng.tensor_tensor(low, hidden[up_lanes(t), t, :], high_of(t), ALU.subtract).then_inc(done, 1)

        def add_ffn(eng, i, r):
            x1 = x_sb[:, bass.ds(i * 2 + r, 1), :]
            wait(eng, out_scaled, 2, i, r + 1)
            eng.tensor_tensor(x1, x1, ffn_out[:, r:r + 1, :], ALU.add).then_inc(out_ready, 1)

        def bank_of(i, t):
            if is_last(i) and t < 4:
                n, half = divmod(t, 2)
                return conv[n][:, half * BANK:(half + 1) * BANK].rearrange("p (n l) -> p n l", n=2)
            return gate_up[t % 2][:, :, :]

        def gate_of(i, t):
            return bank_of(i, t)[gate_lanes(t), 0, :]

        def up_of(i, t):
            return bank_of(i, t)[up_lanes(t), 1 if t < FULL else 0, :]

        def f_parts_of(i):
            return last_f_parts if is_last(i) else f_parts

        block = ctx.enter_context(nc.Block())

        @block.sync
        def _(sp):
            def load_toeplitz(i, s):
                src = bass.AP(taps_pad.tensor, (i * BLOCK_HEADS + s) * (P + L) + 1, [[1, P], [1, L]])
                sp.dma_start(toeplitz[:, s, :], src).then_inc(toeplitz_loaded[s], 16)

            def store(i, r):
                wait(sp, out_ready, 2, i, r + 1)
                sp.dma_start(out_at(i, r), x_at(i, r)).then_inc(out_stored, 16)

            def out_at(i, r):
                return out[bass.ds((i * 2 + r) * P, P), :]

            def x_at(i, r):
                return x_sb[:, bass.ds(i * 2 + r, 1), :]

            sp.dma_start(k_ext[:, 0:1], ctx_ext[:, 0:1]).then_inc(k_loaded[0], 16)
            sp.dma_start(windows[:, 0, :], bass.AP(taps.tensor, 1, [[1, P], [1, L]])).then_inc(windows_loaded[0], 16)
            sp.dma_start(k_ext[:, 1:BLOCK_HEADS], ctx_ext[:, 1:BLOCK_HEADS]).then_inc(k_loaded[1], 16)
            sp.dma_start(windows[:, 1:, :],
                         bass.AP(taps.tensor, P + L + 1, [[1, P], [P + L, BLOCK_HEADS - 1], [1, L]]))\
                .then_inc(windows_loaded[1], 16)
            sp.dma_start(taps_sb[:, :], taps).then_inc(taps_loaded, 16)
            sp.dma_start(skip_sb[:, :], skip).then_inc(taps_loaded, 16)
            heads = slice(BLOCK_HEADS, 2 * BLOCK_HEADS)
            sp.dma_start(k_ext[:, heads], ctx_ext[:, heads]).then_inc(k_loaded[2], 16)
            sp.dma_start(x_sb[:, 2:TILES, :], x[ROWS:, :].rearrange("(t p) l -> p t l", p=P)).then_inc(x_loaded, 16)
            sp.wait_ge(taps_ready, 1)
            sp.dma_start(taps_pad, taps_sb[:, :]).then_inc(taps_stored, 16)
            sp.wait_ge(taps_stored, 16)
            for s in range(BLOCK_HEADS):
                load_toeplitz(1, s)
            sp.dma_start(wg_int[:, :, :], wg_t.rearrange("(c p) n -> p c n", p=P)).then_inc(w_loaded[0], 16)
            sp.dma_start(wu_int[:, :, :], wu_t.rearrange("(c p) n -> p c n", p=P)).then_inc(w_loaded[1], 16)
            heads = slice(2 * BLOCK_HEADS, H)
            sp.dma_start(k_ext[:, heads], ctx_ext[:, heads]).then_inc(k_loaded[3], 16)
            full = FULL * P
            sp.dma_start(wd_int[:, 0:FULL, :],
                         wd_t[0:full, :].rearrange("(t p) n -> p t n", p=P)).then_inc(w_loaded[2], 16)
            for lanes in (gate_lanes(FULL), up_lanes(FULL)):
                sp.dma_start(wd_int[lanes, FULL, :], wd_t[full:HID, :]).then_inc(w_loaded[2], 16)
            sp.dma_start(sg_sb[:, :], s_gate).then_inc(w_loaded[2], 16)
            sp.dma_start(su_sb[:, :], s_up).then_inc(w_loaded[2], 16)
            sp.dma_start(sd_sb[:, :], s_down.partition_broadcast(P)).then_inc(w_loaded[2], 16)

            def reload(i):
                for s in range(BLOCK_HEADS):
                    wait(sp, conv_done, BLOCK_HEADS, i, s + 1)
                    load_toeplitz(i + 1, s)

            with sp.Fori(1, BLOCKS - 1) as i:
                reload(i)
                store(i - 1, 0)
                store(i - 1, 1)
            for i in range(BLOCKS - 2, BLOCKS):
                store(i, 0)
                store(i, 1)
            sp.wait_ge(out_stored, 16 * TILES)

        @block.gpsimd
        def _(pool):
            for semaphore in credited:
                pool.sem_inc(semaphore, 1)
            nc.gpsimd.memset(minus_half[:, :], -0.5).then_inc(half_ready, 1)
            nc.gpsimd.memset(ident[:, :], 0.0).then_inc(ident_zeroed, 1)
            nc.gpsimd.memset(anti[:, :], 0.0).then_inc(ident_zeroed, 1)
            pool.wait_ge(half_ready, 1)
            pool.wait_ge(ident_zeroed, 2)
            nc.gpsimd.affine_select(out=anti[:, :], in_=anti[:, :], compare_op=ALU.not_equal, fill=1.0,
                                    base=1 - P, pattern=[[1, P]], channel_multiplier=1).then_inc(anti_ready, 1)
            nc.gpsimd.affine_select(out=ident[:, :], in_=ident[:, :], compare_op=ALU.not_equal, fill=1.0,
                                    base=0, pattern=[[-1, P]], channel_multiplier=1).then_inc(ident_ready, 1)
            pool.wait_ge(ident_ready, 1)
            nc.gpsimd.tensor_copy(ident16[:, :], ident[:, :]).then_inc(ident_ready, 1)

            def root(base, power, result, done):
                nc.gpsimd.tensor_tensor(result, base, power, ALU.pow).then_inc(done, 1)

            def root_q(i):
                wait(pool, q_variance, 1, i, 1)
                wait(pool, q_normed, 2, i, 0)
                root(variance_q[:, :], minus_half[:, :], rstd_q[:, :], q_rstd)

            def root_f(i, r):
                wait(pool, x1_steps, 8, i, 4 * r + 4)
                wait(pool, f_normed, 2, i, r - 1)
                root(variance_f[:, r:r + 1], minus_half[:, 0:1], rstd_f[:, r:r + 1], f_rstd)

            def merge_slots(i, r):
                z = terms[:, r, :]
                even = view(z, 0, [[TERMS, HALVES], [2 * P, 2], [1, P]])
                odd = view(z, P, [[TERMS, HALVES], [2 * P, 2], [1, P]])
                wait(pool, terms_ready, BLOCK_HEADS, i, 2 * r + 2)
                nc.gpsimd.tensor_tensor(even, even, odd, ALU.add).then_inc(merged, 1)

            def low_hidden(i, t):
                subtract_high(nc.gpsimd, i, t)

            def make(n):
                multiply_pairs(nc.gpsimd, n, made)

            def step(i):
                n = BLOCK_HEADS * i + BLOCK_HEADS
                merge_slots(i, 0)
                low_hidden(i - 1, 0)
                make(n)
                low_hidden(i - 1, 1)
                merge_slots(i, 1)
                make(n + 1)
                root_q(i + 1)
                root_f(i, 0)
                low_hidden(i - 1, 2)
                low_hidden(i - 1, 3)
                root_f(i, 1)
                low_hidden(i - 1, 4)
                make(n + 2)
                make(n + 3)
                add_ffn(nc.gpsimd, i - 1, 0)
                add_ffn(nc.gpsimd, i - 1, 1)

            def last_step(i):
                merge_slots(i, 0)
                low_hidden(i - 1, 0)
                merge_slots(i, 1)
                root_f(i, 0)
                low_hidden(i - 1, 1)
                root_f(i, 1)
                for t in range(2, FULL):
                    low_hidden(i - 1, t)
                add_ffn(nc.gpsimd, i - 1, 0)
                add_ffn(nc.gpsimd, i - 1, 1)

            root_q(0)
            pool.wait_ge(k_loaded[1], 16)
            make(2)
            make(3)
            pool.wait_ge(k_loaded[2], 16)
            make(4)
            merge_slots(0, 0)
            make(5)
            merge_slots(0, 1)
            root_f(0, 0)
            root_q(1)
            make(6)
            root_f(0, 1)
            make(7)
            pool.wait_ge(k_loaded[3], 16)
            with pool.Fori(1, BLOCKS - 1) as i:
                step(i)
            last_step(BLOCKS - 1)

        @block.scalar
        def _(act):
            def evict_q(i, r):
                wait(act, q_turned, 2, i, r + 1)
                wait(act, terms_ready, BLOCK_HEADS, i, 2 * r + 2 - BLOCK_HEADS)
                o, src = q_ext[:, r, :], turn[:, :]
                half, head = EXT * B, HALVES * EXT * B
                nc.scalar.activation(
                    view(o, 0, [[head, TILE_HEADS], [half, HALVES], [1, C * B]]),
                    view(src, 0, [[1, TILE_HEADS], [P, HALVES], [TILE_HEADS, C * B]]), ACT.Copy)
                nc.scalar.activation(
                    view(o, C * B, [[head, TILE_HEADS], [half, HALVES], [1, 4 * B]]),
                    view(src, 0, [[1, TILE_HEADS], [P, HALVES], [TILE_HEADS, 4 * B]]),
                    ACT.Copy).then_inc(q_ready, 1)

            def evict_f(i, r):
                wait(act, f_turned, 2, i, r + 1)
                nc.scalar.activation(f_parts_of(i)[:, :, :, r * P:(r + 1) * P], turn16, ACT.Copy).then_inc(f_ready, 1)

            def gate(i, t):
                wait(act, gate_up_done, CHUNKS, i, t + 1)
                wait_place(act, hidden_ready, CHUNKS, i, t + 1 - CHUNKS)
                nc.scalar.activation(gate_act[up_lanes(t), t, :], gate_of(i, t), ACT.Silu,
                                     scale=sg_sb[gate_lanes(t), t:t + 1]).then_inc(gate_act_ready, 1)

            def hidden_high(i, t):
                wait(act, hidden_ready, CHUNKS, i, t + 1)
                wait_place(act, chunk_down, CHUNKS, i, t + 1 - CHUNKS)
                nc.scalar.activation(high_of(t), hidden[up_lanes(t), t, :], ACT.Copy).then_inc(h_hi_ready, 1)

            def convert(weights, integers):
                return nc.scalar.activation(weights, integers, ACT.Copy, bias=-ZERO_POINT)

            def convert_gate_up():
                act.wait_ge(w_loaded[0], 16)
                convert(wgu[:, :, 0:HID], wg_int[:, :, :])
                act.wait_ge(w_loaded[1], 16)
                convert(wgu[:, :, HID + TAIL:], wu_int[:, :, 0:FULL * P])
                convert(wgu[:, :, HID:HID + TAIL], wu_int[:, :, FULL * P:]).then_inc(w_ready, 1)

            def convert_down():
                act.wait_ge(w_loaded[2], 6 * 16)
                convert(wd[:, :, :], wd_int[:, :, :]).then_inc(w_ready, 1)

            def step(i):
                evict_q(i, 1)
                for t in range(FULL):
                    gate(i - 1, t)
                    if t == 4:
                        evict_q(i + 1, 0)
                    hidden_high(i - 1, t)
                gate(i - 1, FULL)
                evict_f(i, 0)
                hidden_high(i - 1, FULL)
                evict_f(i, 1)

            def last_step(i):
                evict_q(i, 1)
                for t in range(CHUNKS):
                    gate(i - 1, t)
                    if t == 3:
                        evict_f(i, 0)
                    if t == 4:
                        evict_f(i, 1)
                    hidden_high(i - 1, t)

            def last_ffn(i):
                gate(i, 0)
                for t in range(1, CHUNKS):
                    gate(i, t)
                    hidden_high(i, t - 1)
                hidden_high(i, CHUNKS - 1)

            act.dma_start(x_sb[:, 0:2, :], x[0:ROWS, :].rearrange("(t p) l -> p t l", p=P)).then_inc(x0_loaded, 16)
            act.dma_start(skip_all[:, :], skip.rearrange("h a -> (h a)").partition_broadcast(P)).then_inc(skip_loaded, 16)
            nc.scalar.preload_act_table(ACT.Silu)
            evict_q(0, 0)
            evict_q(0, 1)
            convert_gate_up()
            evict_q(1, 0)
            evict_f(0, 0)
            evict_f(0, 1)
            convert_down()
            with act.Fori(1, BLOCKS - 1) as i:
                step(i)
            last_step(BLOCKS - 1)
            last_ffn(BLOCKS - 1)

        @block.vector
        def _(dve):
            dve.memset(zeros[:, :], 0.0).then_inc(zeros_ready, 1)

            def first_window(s):
                dve.scalar_tensor_tensor(out=windows[:, s, 0:P], in0=anti[:, :], scalar=skip_all[:, s:s + 1],
                                         in1=windows[:, s, 0:P], op0=ALU.mult, op1=ALU.add).then_inc(windows_ready, 1)

            def tile_of(i, r):
                return x_sb[:, bass.ds(i * 2 + r, 1), :].rearrange("p t l -> p (t l)")

            def wait_apart(semaphore, per_block, i, offset):
                wait(dve, semaphore, per_block, i, offset)
                dve.sem_inc(waited, 1)

            def variances_q(i):
                for r in range(2):
                    last = dve.bn_stats(stats_q[:, r, :], tile_of(i, r))
                last.then_inc(q_stats, 1)
                wait_apart(q_stats, 1, i, 1)
                for r in range(2):
                    last = dve.bn_aggr(moments_q[:, r, :], stats_q[:, r, :])
                last.then_inc(q_moments, 1)
                wait(dve, q_moments, 1, i, 1)
                dve.tensor_scalar(variance_q[:, :], view(moments_q[:, 0, :], 1, [[2, 2]]), EPS, None,
                                  ALU.add).then_inc(q_variance, 1)

            def norm_q(i, r):
                wait(dve, q_rstd, 1, i, 1)
                wait(dve, q_turned, 2, i, r - 1)
                dve.tensor_scalar(q_rows[:, r, :], tile_of(i, r), moments_q[:, r, 0:1], rstd_q[:, r:r + 1],
                                  ALU.subtract, ALU.mult).then_inc(q_normed, 1)

            def add_sum(i, r):
                x1 = tile_of(i, r)
                wait(dve, summed, 2, i, r + 1)
                dve.tensor_tensor(x1, x1, turn[:, 0:L], ALU.add).then_inc(x1_steps, 1)

            def row_stats(i, r):
                wait_apart(x1_steps, 8, i, 4 * r + 1)
                dve.bn_stats(stats_f[:, r, :], tile_of(i, r)).then_inc(x1_steps, 1)

            def row_moments(i, r):
                wait_apart(x1_steps, 8, i, 4 * r + 2)
                dve.bn_aggr(moments_f[:, r, :], stats_f[:, r, :]).then_inc(x1_steps, 1)

            def row_variance(i, r):
                wait(dve, x1_steps, 8, i, 4 * r + 3)
                dve.tensor_scalar(variance_f[:, r:r + 1], moments_f[:, r, 1:2], EPS, None,
                                  ALU.add).then_inc(x1_steps, 1)

            def norm_rows(i, r):
                wait(dve, f_rstd, 2, i, r + 1)
                dve.tensor_scalar(f_rows[:, r, :], tile_of(i, r), moments_f[:, r, 0:1], rstd_f[:, r:r + 1],
                                  ALU.subtract, ALU.mult).then_inc(f_steps, 1)

            def high_rows(i, r):
                wait(dve, f_steps, 4, i, 2 * r + 1)
                wait(dve, f_turned, 2, i, r - 1)
                dve.tensor_copy(f_row_parts[:, r, 0, :], f_rows[:, r, :]).then_inc(f_steps, 1)

            def low_rows(i, r):
                wait(dve, f_steps, 4, i, 2 * r + 2)
                dve.tensor_tensor(f_row_parts[:, r, 1, :], f_rows[:, r, :], f_row_parts[:, r, 0, :],
                                  ALU.subtract).then_inc(f_normed, 1)

            def add_attention(i, r):
                add_sum(i, r)
                row_stats(i, r)
                row_moments(i, r)
                row_variance(i, r)

            def norm_f(i, r):
                norm_rows(i, r)
                high_rows(i, r)
                low_rows(i, r)

            def norm_f_and_add_attention(i):
                norm_rows(i, 0)
                add_sum(i, 1)
                high_rows(i, 0)
                row_stats(i, 1)
                low_rows(i, 0)
                row_moments(i, 1)
                row_variance(i, 1)

            def multiply_terms(i, s):
                r, h = s // TILE_HEADS, s % TILE_HEADS
                wait(dve, conv_done, BLOCK_HEADS, i, s + 1)
                if h == 0:
                    wait(dve, q_ready, 2, i, r + 1)
                    wait(dve, summed, 2, i, r - 1)
                y = conv[s % 2][:, :]
                q = q_ext[:, r, :]
                z = terms[:, r, :]
                half = EXT * B
                q0 = h * HALVES * half
                to = TILE_HEADS
                dve.tensor_tensor(view(z, h, [[TERMS, HALVES], [P, 4], [to, C * B]]),
                                  view(y, HALF0, [[COLS, HALVES], [C * B, 4], [1, C * B]]),
                                  view(q, q0, [[half, HALVES], [B, 4], [1, C * B]]), ALU.mult)
                dve.tensor_tensor(view(z, h + BACK + CHANNEL,
                                       [[TERMS, HALVES], [P + SPARE + CHANNEL, 3], [to, C * B]]),
                                  view(y, HALF0 + C * B, [[COLS, HALVES], [C * B, 3], [1, C * B]]),
                                  view(q, q0, [[half, HALVES], [0, 3], [1, C * B]]), ALU.mult)
                dve.tensor_tensor(view(z, h + BACK - 2 * CHANNEL,
                                       [[TERMS, HALVES], [P + SPARE + CHANNEL, 3], [to, 3 * B]]),
                                  view(y, HALF0 + (C + 5) * B, [[COLS, HALVES], [C * B, 3], [1, 3 * B]]),
                                  view(q, q0 + 5 * B, [[half, HALVES], [0, 3], [1, 3 * B]]), ALU.mult)
                dve.tensor_tensor(view(z, h + CROSS, [[TERMS, HALVES], [4 * CHANNEL, 2], [to, 4 * B]]),
                                  view(y, HALF0 + 4 * C * B, [[COLS, HALVES], [0, 2], [1, 4 * B]]),
                                  view(q, q0 + 4 * B, [[half, HALVES], [4 * B, 2], [1, 4 * B]]),
                                  ALU.mult).then_inc(terms_ready, 1)

            def hidden_units(i, t):
                wait(dve, gate_act_ready, CHUNKS, i, t + 1)
                if t < FULL:
                    wait_place(dve, h_lo_ready, FULL, i, t + 1 - FULL)
                lanes = up_lanes(t)
                dve.scalar_tensor_tensor(out=hidden[lanes, t, :], in0=up_of(i, t), scalar=su_sb[lanes, t:t + 1],
                                         in1=gate_act[lanes, t, :], op0=ALU.mult,
                                         op1=ALU.mult).then_inc(hidden_ready, 1)

            def scale_out(i):
                wait(dve, chunk_down, CHUNKS, i, CHUNKS)
                for r in range(2):
                    wait_place(dve, out_ready, 2, i, r - 1)
                    dve.tensor_tensor(ffn_out[:, r, :], down[:, r, :], sd_sb[:, :],
                                      ALU.mult).then_inc(out_scaled, 1)

            def first_step():
                multiply_terms(0, 2)
                multiply_terms(0, 3)
                add_attention(0, 0)
                dve.wait_ge(x_loaded, 16)
                variances_q(1)
                norm_rows(0, 0)
                add_sum(0, 1)
                high_rows(0, 0)
                row_stats(0, 1)
                low_rows(0, 0)
                row_moments(0, 1)
                row_variance(0, 1)
                norm_q(1, 0)
                norm_q(1, 1)
                norm_f(0, 1)
                multiply_terms(1, 0)
                multiply_terms(1, 1)

            def step(i):
                hidden_units(i - 1, 0)
                multiply_terms(i, 2)
                hidden_units(i - 1, 1)
                multiply_terms(i, 3)
                hidden_units(i - 1, 2)
                variances_q(i + 1)
                add_attention(i, 0)
                hidden_units(i - 1, 3)
                norm_q(i + 1, 0)
                norm_f_and_add_attention(i)
                hidden_units(i - 1, 4)
                norm_q(i + 1, 1)
                norm_f(i, 1)
                hidden_units(i - 1, 5)
                multiply_terms(i + 1, 0)
                subtract_high(dve, i - 1, 5)
                multiply_terms(i + 1, 1)
                scale_out(i - 1)

            def last_step(i):
                hidden_units(i - 1, 0)
                multiply_terms(i, 2)
                multiply_terms(i, 3)
                add_attention(i, 0)
                hidden_units(i - 1, 1)
                norm_f_and_add_attention(i)
                hidden_units(i - 1, 2)
                norm_f(i, 1)
                for t in range(3, CHUNKS):
                    hidden_units(i - 1, t)
                subtract_high(dve, i - 1, 5)

            def last_ffn(i):
                hidden_units(i, 0)
                for t in range(1, CHUNKS):
                    hidden_units(i, t)
                    subtract_high(dve, i, t - 1)
                    if t == 1:
                        scale_out(i - 1)
                subtract_high(dve, i, CHUNKS - 1)
                scale_out(i)
                for r in range(2):
                    add_ffn(dve, i, r)

            dve.wait_ge(k_loaded[0], 16)
            multiply_pairs(dve, 0, first_made)
            dve.wait_ge(x0_loaded, 16)
            variances_q(0)
            dve.wait_ge(windows_loaded[0], 16)
            dve.wait_ge(skip_loaded, 16)
            dve.wait_ge(anti_ready, 1)
            first_window(0)
            dve.wait_ge(k_loaded[1], 16)
            multiply_pairs(dve, 1, first_made)
            dve.wait_ge(windows_loaded[1], 16)
            first_window(1)
            norm_q(0, 0)
            norm_q(0, 1)
            first_window(2)
            first_window(3)
            dve.wait_ge(taps_loaded, 32)
            dve.tensor_tensor(taps_sb[:, P:P + 1], taps_sb[:, P:P + 1], skip_sb[:, :], ALU.add).then_inc(taps_ready, 1)
            multiply_terms(0, 0)
            multiply_terms(0, 1)
            first_step()
            with dve.Fori(1, BLOCKS - 1) as i:
                step(i)
            last_step(BLOCKS - 1)
            last_ffn(BLOCKS - 1)

        @block.tensor
        def _(pe):
            def turn_q(i, r):
                wait(pe, q_normed, 2, i, r + 1)
                if r == 0:
                    wait(pe, x1_steps, 8, i, -3)
                else:
                    wait(pe, q_ready, 2, i, 1)
                    wait(pe, f_ready, 2, i, 0)
                for c in range(HALVES):
                    last = nc.tensor.transpose(turn[:, c * P:(c + 1) * P], q_rows[:, r, c * P:(c + 1) * P],
                                               ident[:, :])
                last.then_inc(q_turned, 1)

            def turn_f(i, r):
                wait(pe, f_normed, 2, i, r + 1)
                if r == 1:
                    wait(pe, f_ready, 2, i, 1)
                elif is_last(i):
                    wait(pe, x1_steps, 8, i, 5)
                else:
                    wait(pe, q_ready, 2, i, 3)
                for part in range(2):
                    for c in range(HALVES):
                        last = nc.tensor.transpose(turn16[:, part, c, :],
                                                   f_row_parts[:, r, part, c * P:(c + 1) * P], ident16[:, :])
                last.then_inc(f_turned, 1)

            def convolve(i, s):
                if isinstance(i, int) and i == 0:
                    if s < 2:
                        pe.wait_ge(first_made, s + 1)
                    else:
                        pe.wait_ge(made, s - 1)
                    pe.wait_ge(windows_ready, s + 1)
                else:
                    wait(pe, made, BLOCK_HEADS, i, s - 1)
                    wait(pe, toeplitz_loaded[s], 16, i, 0)
                wait(pe, terms_ready, BLOCK_HEADS, i, s - 1)
                y = conv[s % 2]
                halves = [products[:, bass.ds(i * BLOCK_HEADS + s, 1), c * COLS:(c + 1) * COLS]
                          .rearrange("p h n -> p (h n)") for c in range(HALVES)]
                matrix = windows if isinstance(i, int) and i == 0 else toeplitz
                within, across = matrix[:, s, 0:P], matrix[:, s, P:L]
                nc.tensor.matmul(y[:, HALF0:BANK], within, halves[0], start=True, stop=True)
                nc.tensor.matmul(y[:, BANK:BANK + COLS], within, halves[1], start=True, stop=False)
                nc.tensor.matmul(y[:, BANK:BANK + COLS], across, halves[0], start=False,
                                 stop=True).then_inc(conv_done, 1)

            def sum_terms(i, r):
                wait(pe, merged, 2, i, r + 1)
                if r == 0:
                    wait(pe, q_ready, 2, i, 2)
                else:
                    wait(pe, x1_steps, 8, i, 1)
                z = terms[:, r, :]
                for c in range(HALVES):
                    for n, slot in enumerate(SUMMED_SLOTS):
                        cols = view(z, c * TERMS + slot, [[1, P]])
                        last = nc.tensor.matmul(turn[:, c * P:(c + 1) * P], cols, ident[:, :],
                                                is_transpose=True, start=(n == 0),
                                                stop=(n == len(SUMMED_SLOTS) - 1))
                last.then_inc(summed, 1)

            def gates(i, t):
                if t == 0:
                    wait(pe, f_ready, 2, i, 2)
                if not is_last(i):
                    wait_place(pe, hidden_ready, CHUNKS, i, t - 1)
                elif t >= 4:
                    wait(pe, hidden_ready, CHUNKS, i, t + 1 - CHUNKS)
                starts = (t * P, HID + TAIL + t * P) if t < FULL else (t * P,)
                for n, column in enumerate(starts):
                    for c in range(HALVES):
                        for part in range(2):
                            last = nc.tensor.matmul(bank_of(i, t)[:, n, :], wgu[:, c, column:column + P],
                                                    f_parts_of(i)[:, part, c, :], start=(c == 0 and part == 0),
                                                    stop=(c == HALVES - 1 and part == 1))
                last.then_inc(gate_up_done, 1)

            def downs(i, t):
                if t == FULL:
                    wait(pe, tail_ready, 1, i, 1)
                elif is_last(i):
                    pe.wait_ge(last_h_lo_ready, t + 1)
                else:
                    wait(pe, h_lo_ready, FULL, i, t + 1)
                if t == 0:
                    pe.wait_ge(w_ready, 2)
                    wait_place(pe, out_scaled, 2, i, 0)
                parts = (h_hi[:, t, :], h_lo[:, t, :]) if t < FULL else (h_tail[:, :],)
                for r in range(2):
                    for n, part in enumerate(parts):
                        last = nc.tensor.matmul(down[:, r, :], part[:, r * P:(r + 1) * P], wd[:, t, :],
                                                start=(t == 0 and r == 0 and n == 0),
                                                stop=(t == FULL), skip_group_check=True)
                last.then_inc(chunk_down, 1)

            def fill(bank, count):
                for n in range(count):
                    nc.tensor.matmul(bank, zeros[:, 0:P], zeros[:, :], start=True, stop=True)

            def first_step():
                convolve(0, 0)
                pe.wait_ge(ident_ready, 2)
                turn_q(0, 0)
                convolve(0, 1)
                turn_q(0, 1)
                fill(down[:, 0, :], FILL)
                convolve(0, 2)
                convolve(0, 3)
                sum_terms(0, 0)
                convolve(1, 0)
                sum_terms(0, 1)
                convolve(1, 1)
                fill(down[:, 0, :], FILL)
                turn_q(1, 0)
                fill(down[:, 0, :], FILL)
                turn_f(0, 0)
                fill(down[:, 0, :], FILL)
                turn_f(0, 1)
                fill(down[:, 0, :], FILL)

            def step(i):
                turn_q(i, 1)
                gates(i - 1, 0)
                convolve(i, 2)
                gates(i - 1, 1)
                convolve(i, 3)
                gates(i - 1, 2)
                downs(i - 1, 0)
                sum_terms(i, 0)
                gates(i - 1, 3)
                downs(i - 1, 1)
                sum_terms(i, 1)
                gates(i - 1, 4)
                turn_q(i + 1, 0)
                downs(i - 1, 2)
                gates(i - 1, 5)
                convolve(i + 1, 0)
                turn_f(i, 0)
                downs(i - 1, 3)
                downs(i - 1, 4)
                turn_f(i, 1)
                convolve(i + 1, 1)
                downs(i - 1, 5)

            def last_step(i):
                turn_q(i, 1)
                gates(i - 1, 0)
                convolve(i, 2)
                convolve(i, 3)
                sum_terms(i, 0)
                gates(i - 1, 1)
                sum_terms(i, 1)
                gates(i - 1, 2)
                downs(i - 1, 0)
                gates(i - 1, 3)
                downs(i - 1, 1)
                turn_f(i, 0)
                gates(i - 1, 4)
                downs(i - 1, 2)
                turn_f(i, 1)
                gates(i - 1, 5)
                downs(i - 1, 3)
                gates(i, 0)
                downs(i - 1, 4)
                gates(i, 1)
                downs(i - 1, 5)

            def last_ffn(i):
                for t in range(2, CHUNKS):
                    gates(i, t)
                for t in range(CHUNKS):
                    downs(i, t)

            pe.wait_ge(zeros_ready, 1)
            fill(turn[:, 0:2 * P], FILL_START)
            first_step()
            pe.wait_ge(w_ready, 1)
            with pe.Fori(1, BLOCKS - 1) as i:
                step(i)
            last_step(BLOCKS - 1)
            last_ffn(BLOCKS - 1)


def kernel(x, ctx_2048, L0_xattn_ssm_kernel, L0_xattn_D, L0_ffn_wq_gate, L0_ffn_s_gate, L0_ffn_wq_up,
           L0_ffn_s_up, L0_ffn_wq_down, L0_ffn_s_down):
    import numpy as np
    import concourse.bacc as bacc
    from concourse.bass_utils import run_bass_kernel_spmd

    rows = np.asarray(x).reshape(B, TILES, TILE_HEADS, C, L).transpose(1, 3, 0, 2, 4).reshape(TILES * P, L)
    k = np.asarray(ctx_2048).reshape(B, H, C, HALVES, P)[..., ::-1].transpose(4, 1, 3, 2, 0)
    k = np.concatenate([k, k[:, :, :, :4]], axis=3).reshape(P, H, HALVES, EXT * B)

    taps = np.zeros((H, P + L), np.asarray(L0_xattn_ssm_kernel).dtype)
    taps[:, P:] = np.asarray(L0_xattn_ssm_kernel)

    def columns(s, lanes):
        s = np.asarray(s)
        placed = np.zeros((P, CHUNKS), s.dtype)
        placed[:, :FULL] = s[:FULL * P].reshape(FULL, P).T
        placed[lanes, FULL] = s[FULL * P:]
        return placed

    arrays = {
        "x": rows,
        "ctx_ext": k,
        "taps": taps,
        "skip": np.asarray(L0_xattn_D).reshape(H, 1),
        "wg_t": np.asarray(L0_ffn_wq_gate).T,
        "s_gate": columns(L0_ffn_s_gate, gate_lanes(FULL)),
        "wu_t": np.asarray(L0_ffn_wq_up).T,
        "s_up": columns(L0_ffn_s_up, up_lanes(FULL)),
        "wd_t": np.asarray(L0_ffn_wq_down).T,
        "s_down": np.asarray(L0_ffn_s_down),
    }
    arrays = {name: np.ascontiguousarray(a) for name, a in arrays.items()}

    nc = bacc.Bacc("TRN2", target_bir_lowering=False, num_devices=1)
    args = [nc.dram_tensor(name, a.shape, mybir.dt.from_np(a.dtype), kind="ExternalInput").ap()
            for name, a in arrays.items()]
    taps_pad = nc.dram_tensor("taps_pad", (H, P + L), F32).ap()
    out = nc.dram_tensor("out", (H * B * C, L), F32, kind="ExternalOutput").ap()
    build(nc, *args, taps_pad, out)
    got = run_bass_kernel_spmd(nc, [arrays], core_ids=[0]).results[0]["out"]
    return np.asarray(got).reshape(TILES, C, B, TILE_HEADS, L).transpose(2, 0, 3, 1, 4).reshape(B, H * C, L)
```
